# Optimizing a Trainium2 kernel written in Bass

```python
import numpy as np
import jax
import jax.numpy as jnp

def _softmax(x, axis=-1):
    return jax.nn.softmax(x, axis=axis)

def _gelu(x):
    return jax.nn.gelu(x, approximate=True)

def _silu(x):
    return jax.nn.silu(x)

def _sigmoid(x):
    return jax.nn.sigmoid(x)

def _layernorm(x, axis=-1, eps=1e-05):
    m = jnp.mean(x, axis=axis, keepdims=True)
    v = jnp.var(x, axis=axis, keepdims=True)
    return (x - m) / jnp.sqrt(v + eps)

def _scatter_add(tgt, idx, src, axis=0):
    return tgt.at[idx].add(src)

def _segment_sum(src, seg, n):
    return jax.ops.segment_sum(src, seg, n)
kernel_name = 'mk_dlrm_tower_d1_rec_r8_af7612'

def setup_inputs(seed: int=0):
    np.random.seed(seed)
    _w = jnp.asarray

    def _rec_inputs():
        import jax
        import jax.numpy as jnp
        _tk = jax.random.key(seed)
        ids = jnp.stack([jax.random.randint(jax.random.fold_in(_tk, 200 + f), (2048,), 0, v, jnp.int32) for f, v in enumerate([1000, 1000, 1000, 125000, 1250, 1000, 1000, 12500, 1000, 1250, 12500, 1000, 1250, 1250, 12500, 12500, 1250, 12500, 1000, 1000, 1250, 12500, 12500, 12500, 1250, 1250])], axis=1)
        tbl_0 = 0.05 * jax.random.normal(jax.random.fold_in(_tk, 500 + 0), (1000, 128), jnp.float32)
        tbl_1 = 0.05 * jax.random.normal(jax.random.fold_in(_tk, 500 + 1), (1000, 128), jnp.float32)
        tbl_2 = 0.05 * jax.random.normal(jax.random.fold_in(_tk, 500 + 2), (1000, 128), jnp.float32)
        tbl_3 = 0.05 * jax.random.normal(jax.random.fold_in(_tk, 500 + 3), (125000, 128), jnp.float32)
        tbl_4 = 0.05 * jax.random.normal(jax.random.fold_in(_tk, 500 + 4), (1250, 128), jnp.float32)
        tbl_5 = 0.05 * jax.random.normal(jax.random.fold_in(_tk, 500 + 5), (1000, 128), jnp.float32)
        tbl_6 = 0.05 * jax.random.normal(jax.random.fold_in(_tk, 500 + 6), (1000, 128), jnp.float32)
        tbl_7 = 0.05 * jax.random.normal(jax.random.fold_in(_tk, 500 + 7), (12500, 128), jnp.float32)
        tbl_8 = 0.05 * jax.random.normal(jax.random.fold_in(_tk, 500 + 8), (1000, 128), jnp.float32)
        tbl_9 = 0.05 * jax.random.normal(jax.random.fold_in(_tk, 500 + 9), (1250, 128), jnp.float32)
        tbl_10 = 0.05 * jax.random.normal(jax.random.fold_in(_tk, 500 + 10), (12500, 128), jnp.float32)
        tbl_11 = 0.05 * jax.random.normal(jax.random.fold_in(_tk, 500 + 11), (1000, 128), jnp.float32)
        tbl_12 = 0.05 * jax.random.normal(jax.random.fold_in(_tk, 500 + 12), (1250, 128), jnp.float32)
        tbl_13 = 0.05 * jax.random.normal(jax.random.fold_in(_tk, 500 + 13), (1250, 128), jnp.float32)
        tbl_14 = 0.05 * jax.random.normal(jax.random.fold_in(_tk, 500 + 14), (12500, 128), jnp.float32)
        tbl_15 = 0.05 * jax.random.normal(jax.random.fold_in(_tk, 500 + 15), (12500, 128), jnp.float32)
        tbl_16 = 0.05 * jax.random.normal(jax.random.fold_in(_tk, 500 + 16), (1250, 128), jnp.float32)
        tbl_17 = 0.05 * jax.random.normal(jax.random.fold_in(_tk, 500 + 17), (12500, 128), jnp.float32)
        tbl_18 = 0.05 * jax.random.normal(jax.random.fold_in(_tk, 500 + 18), (1000, 128), jnp.float32)
        tbl_19 = 0.05 * jax.random.normal(jax.random.fold_in(_tk, 500 + 19), (1000, 128), jnp.float32)
        tbl_20 = 0.05 * jax.random.normal(jax.random.fold_in(_tk, 500 + 20), (1250, 128), jnp.float32)
        tbl_21 = 0.05 * jax.random.normal(jax.random.fold_in(_tk, 500 + 21), (12500, 128), jnp.float32)
        tbl_22 = 0.05 * jax.random.normal(jax.random.fold_in(_tk, 500 + 22), (12500, 128), jnp.float32)
        tbl_23 = 0.05 * jax.random.normal(jax.random.fold_in(_tk, 500 + 23), (12500, 128), jnp.float32)
        tbl_24 = 0.05 * jax.random.normal(jax.random.fold_in(_tk, 500 + 24), (1250, 128), jnp.float32)
        tbl_25 = 0.05 * jax.random.normal(jax.random.fold_in(_tk, 500 + 25), (1250, 128), jnp.float32)
        _rk = jax.random.fold_in(_tk, 7)
        r_dense_features = -0.000520686 + 1.00062 * jax.random.normal(jax.random.fold_in(_rk, 101), (2048, 128), jnp.float32)
        W_top1 = 0.0405887 * jax.random.normal(jax.random.fold_in(_tk, 801), (607, 512), jnp.float32)
        W_top2 = 0.0441942 * jax.random.normal(jax.random.fold_in(_tk, 802), (512, 256), jnp.float32)
        W_top3 = 0.0625 * jax.random.normal(jax.random.fold_in(_tk, 803), (256, 1), jnp.float32)
        b_top1 = jnp.zeros((512,), jnp.float32)
        b_top2 = jnp.zeros((256,), jnp.float32)
        return (r_dense_features, ids, tbl_0, tbl_1, tbl_2, tbl_3, tbl_4, tbl_5, tbl_6, tbl_7, tbl_8, tbl_9, tbl_10, tbl_11, tbl_12, tbl_13, tbl_14, tbl_15, tbl_16, tbl_17, tbl_18, tbl_19, tbl_20, tbl_21, tbl_22, tbl_23, tbl_24, tbl_25, W_top1, b_top1, W_top2, b_top2, W_top3)
    r_dense_features, ids, tbl_0, tbl_1, tbl_2, tbl_3, tbl_4, tbl_5, tbl_6, tbl_7, tbl_8, tbl_9, tbl_10, tbl_11, tbl_12, tbl_13, tbl_14, tbl_15, tbl_16, tbl_17, tbl_18, tbl_19, tbl_20, tbl_21, tbl_22, tbl_23, tbl_24, tbl_25, W_top1, b_top1, W_top2, b_top2, W_top3 = _rec_inputs()

    def _L0_rec_setup():
        import jax, jax.numpy as jnp
        import numpy as np
        NUM_SPARSE = 26
        EMBED_DIM = 128
        BATCH = 2048
        key = jax.random.key(seed)
        k1, k2 = jax.random.split(key)
        dense_features = jax.random.normal(k1, (BATCH, EMBED_DIM), dtype=jnp.float32)
        sparse_features = jax.random.normal(k2, (BATCH, NUM_SPARSE, EMBED_DIM), dtype=jnp.float32)
        return {'dense_features': dense_features, 'sparse_features': sparse_features}
    _L0_rec_all = _L0_rec_setup()
    _L0_rec_in = {k: v for k, v in _L0_rec_all.items() if k in ()}
    del _L0_rec_all
    return {'r_dense_features': r_dense_features, 'ids': ids, 'tbl_0': tbl_0, 'tbl_1': tbl_1, 'tbl_2': tbl_2, 'tbl_3': tbl_3, 'tbl_4': tbl_4, 'tbl_5': tbl_5, 'tbl_6': tbl_6, 'tbl_7': tbl_7, 'tbl_8': tbl_8, 'tbl_9': tbl_9, 'tbl_10': tbl_10, 'tbl_11': tbl_11, 'tbl_12': tbl_12, 'tbl_13': tbl_13, 'tbl_14': tbl_14, 'tbl_15': tbl_15, 'tbl_16': tbl_16, 'tbl_17': tbl_17, 'tbl_18': tbl_18, 'tbl_19': tbl_19, 'tbl_20': tbl_20, 'tbl_21': tbl_21, 'tbl_22': tbl_22, 'tbl_23': tbl_23, 'tbl_24': tbl_24, 'tbl_25': tbl_25, 'W_top1': W_top1, 'b_top1': b_top1, 'W_top2': W_top2, 'b_top2': b_top2, 'W_top3': W_top3}

def reference(r_dense_features, ids, tbl_0, tbl_1, tbl_2, tbl_3, tbl_4, tbl_5, tbl_6, tbl_7, tbl_8, tbl_9, tbl_10, tbl_11, tbl_12, tbl_13, tbl_14, tbl_15, tbl_16, tbl_17, tbl_18, tbl_19, tbl_20, tbl_21, tbl_22, tbl_23, tbl_24, tbl_25, W_top1, b_top1, W_top2, b_top2, W_top3):
    import jax
    import jax.numpy as jnp

    def _L0_rec_ref(dense_features, sparse_features):
        import jax, jax.numpy as jnp
        import numpy as np
        NUM_SPARSE = 26
        EMBED_DIM = 128
        BATCH = 2048
        F = NUM_SPARSE + 1
        combined = jnp.concatenate([dense_features[:, None, :], sparse_features], axis=1)
        interactions = jnp.einsum('bfd,bgd->bfg', combined, combined)
        iu, ju = jnp.triu_indices(F, k=1)
        interactions_flat = interactions[:, iu, ju]
        return jnp.concatenate([dense_features, interactions_flat], axis=1)
    e = jnp.stack([tbl_0[ids[:, 0]], tbl_1[ids[:, 1]], tbl_2[ids[:, 2]], tbl_3[ids[:, 3]], tbl_4[ids[:, 4]], tbl_5[ids[:, 5]], tbl_6[ids[:, 6]], tbl_7[ids[:, 7]], tbl_8[ids[:, 8]], tbl_9[ids[:, 9]], tbl_10[ids[:, 10]], tbl_11[ids[:, 11]], tbl_12[ids[:, 12]], tbl_13[ids[:, 13]], tbl_14[ids[:, 14]], tbl_15[ids[:, 15]], tbl_16[ids[:, 16]], tbl_17[ids[:, 17]], tbl_18[ids[:, 18]], tbl_19[ids[:, 19]], tbl_20[ids[:, 20]], tbl_21[ids[:, 21]], tbl_22[ids[:, 22]], tbl_23[ids[:, 23]], tbl_24[ids[:, 24]], tbl_25[ids[:, 25]]], axis=1)
    z = _L0_rec_ref(r_dense_features, e)
    z = z.reshape(z.shape[0], -1)
    h = jnp.concatenate([z, r_dense_features], axis=1)
    h = jnp.maximum(h @ W_top1 + b_top1, 0.0)
    h = jnp.maximum(h @ W_top2 + b_top2, 0.0)
    y = h @ W_top3
    return y

_drawn_inputs = setup_inputs


def setup_inputs(seed=0):
    import zlib

    import numpy as np

    out = dict(_drawn_inputs(seed))
    spreads = {'b_top1': (0.0, 0.1), 'b_top2': (0.0, 0.1)}
    factors = {}
    for name, (base, spread) in spreads.items():
        noise = np.random.default_rng([zlib.crc32(name.encode()), seed]).standard_normal(out[name].shape)
        drawn = base * np.exp(spread * noise) if base else spread * noise
        out[name] = jnp.asarray(drawn.astype(out[name].dtype))
    for name, factor in factors.items():
        out[name] = (out[name] * factor).astype(out[name].dtype)
    return out
```

```python
import concourse.bass as bass
from concourse import mybir
from contextlib import ExitStack

BATCH = 2048
EMBED = 128
VOCAB = [1000, 1000, 1000, 125000, 1250, 1000, 1000, 12500, 1000, 1250, 12500, 1000, 1250,
         1250, 12500, 12500, 1250, 12500, 1000, 1000, 1250, 12500, 12500, 12500, 1250, 1250]
SPARSE = len(VOCAB)
FEATURES = SPARSE + 1
PAIRS = FEATURES * (FEATURES - 1) // 2
HIDDEN1, HIDDEN2 = 512, 256

ONE_HOT = 6
ROWS = 1000
ROW_PARTS = 125
ROW_CHUNKS = ROWS // ROW_PARTS
ONE_HOT_TABLES = [f for f, v in enumerate(VOCAB) if v == ROWS][:ONE_HOT]
GATHER_TABLES = [f for f in range(SPARSE) if f not in ONE_HOT_TABLES]
GATHERED = len(GATHER_TABLES)
SLOTS = 1 + GATHERED
FEATURE_ORDER = [0] + [1 + f for f in GATHER_TABLES] + [1 + f for f in ONE_HOT_TABLES]

TILE = 128
SLAB_TILES = 2
SLAB = TILE * SLAB_TILES
SLABS = BATCH // SLAB
GROUP = 4
BLOCK = GROUP * FEATURES
QUARTER = TILE // GROUP
GROUPS = SLAB_TILES * QUARTER

REACH = FEATURES // 2
PAIR_ROWS = [(FEATURES + 1) * f + k for f in range(FEATURES - 1) for k in range(1, REACH + 1)]
PAIR_ROWS += [(FEATURES + 1) * f + REACH + 1 for f in range(REACH)]
PAIR_CHUNK = 9 * REACH
PAIR_CHUNKS = PAIRS // PAIR_CHUNK


def triu_index(a, b):
    return a * FEATURES - a * (a + 1) // 2 + b - a - 1


def pair_weights_order():
    order = []
    for row in PAIR_ROWS:
        a, b = FEATURE_ORDER[row // FEATURES], FEATURE_ORDER[row % FEATURES]
        order.append(triu_index(min(a, b), max(a, b)))
    return order


LOOKUP_BANKS, GRAM_BANKS, MLP_BANKS = 3, 3, 2
PER_BANK = 4
HOT_FILLS = ONE_HOT // 2
TILE_FILLS = -(-SLOTS // PER_BANK)
LOOKUP_FILLS = HOT_FILLS + SLAB_TILES * TILE_FILLS
GRAM_TILE_FILLS = QUARTER // 4
GRAM_FILLS = SLAB_TILES * GRAM_TILE_FILLS
MLP_FILLS = HIDDEN1 // 128 + HIDDEN2 // 128 + 1
assert ONE_HOT % 2 == 0 and HOT_FILLS % 2 == 1 and TILE_FILLS % 2 == 0


FIRST, LAST = (0, 0), (0, SLABS - 1)


def is_first(slab):
    return isinstance(slab[0], int) and sum(slab) == 0


def later(slab, n):
    return slab[0], slab[1] + n


def total(slab, per, n=0):
    base = slab[1] * per + n
    return base if isinstance(slab[0], int) else slab[0] * per + base


def by_vector(fill):
    return fill % 2 == 1


def emptied(fill, vector):
    return sum(by_vector(i) == vector for i in range(fill + 1))


def previous_user(fill, fills, banks):
    if fill >= banks:
        return 0, fill - banks
    return 1, max(i for i in range(fills) if i % banks == fill % banks)


def build(nc, dense, ids, hot_ids, tables, w_inter, w_dense, b1, w2, b2, w3, out):
    f32, i32 = mybir.dt.float32, mybir.dt.int32
    bf16, f16 = mybir.dt.bfloat16, mybir.dt.float16
    ALU, ACT = mybir.AluOpType, mybir.ActivationFunctionType
    H1C, H2C = HIDDEN1 // 128, HIDDEN2 // 128

    with ExitStack() as ctx:
        def sb(name, shape, dt):
            return ctx.enter_context(nc.sbuf_tensor(name, shape, dt))

        def sem(name):
            return ctx.enter_context(nc.semaphore(name))

        idx = [sb(f"idx{h}", [TILE, SPARSE], i32) for h in range(SLAB_TILES)]
        rows = [sb(f"rows{h}", [TILE, SLOTS * EMBED], f32) for h in range(SLAB_TILES)]
        emb = sb("emb", [EMBED, SLAB_TILES, TILE, FEATURES], f32)
        hot_ids_i = sb("hot_ids_i", [128, ONE_HOT, SLAB], i32)
        hot_ids_h = sb("hot_ids_h", [128, ONE_HOT, SLAB], f16)
        row_number = sb("row_number", [128, ROW_CHUNKS], f32)
        hot = [sb(f"hot{t}", [128, ROW_CHUNKS, SLAB], bf16) for t in range(ONE_HOT)]
        part = [[sb(f"part{t}_{k}", [ROW_PARTS, ROW_CHUNKS, EMBED], bf16) for k in range(3)]
                for t in range(ONE_HOT)]
        stage = sb("stage", [128, BLOCK * GROUPS], f32)
        stage_v = stage[:, :].rearrange("p (c h q) -> p c h q", c=BLOCK, h=SLAB_TILES)
        raw_cols = ROW_CHUNKS * EMBED
        raw = [stage[0:ROW_PARTS, t * raw_cols:(t + 1) * raw_cols] for t in range(ONE_HOT)]
        assert ONE_HOT * raw_cols <= BLOCK * GROUPS
        dense_t = sb("dense_t", [EMBED, GROUP, SLAB_TILES, QUARTER], f32)
        inter = sb("inter", [PAIR_CHUNK, PAIR_CHUNKS, SLAB], f32)
        h1 = sb("h1", [128, H1C, SLAB], f32)
        h2 = sb("h2", [128, H2C, SLAB], f32)
        y = sb("y", [128, SLABS * SLAB_TILES], f32)
        w1p = sb("w1p", [PAIR_CHUNK, PAIR_CHUNKS, HIDDEN1], f32)
        w1d2 = sb("w1d2", [EMBED, 2, HIDDEN1], f32)
        w1d = sb("w1d", [EMBED, HIDDEN1], f32)
        w2s = sb("w2s", [128, H1C, HIDDEN2], f32)
        w3s = sb("w3s", [128, H2C], f32)
        b1s = sb("b1s", [128, H1C], f32)
        b2s = sb("b2s", [128, H2C], f32)
        ident = sb("ident", [128, 128], f32)
        scratch = nc.dram_tensor("pair_products", (FEATURES * FEATURES, SLAB), f32, kind="Internal").ap()

        lookup = [ctx.enter_context(nc.psum_tensor(f"lookup{i}", [128, 512], f32)) for i in range(LOOKUP_BANKS)]
        gram = [ctx.enter_context(nc.psum_tensor(f"gram{i}", [128, 512], f32)) for i in range(GRAM_BANKS)]
        mlp = [ctx.enter_context(nc.psum_tensor(f"mlp{i}", [128, 512], f32)) for i in range(MLP_BANKS)]

        idx_loaded = [sem(f"idx_loaded{h}") for h in range(SLAB_TILES)]
        dense_loaded = [sem(f"dense_loaded{h}") for h in range(SLAB_TILES)]
        gathered = [sem(f"gathered{h}") for h in range(SLAB_TILES)]
        raw_loaded = [sem(f"raw_loaded{t}") for t in range(ONE_HOT)]
        weights_loaded = sem("weights_loaded")
        hot_ids_loaded = sem("hot_ids_loaded")
        hot_ids_converted = sem("hot_ids_converted")
        row_number_made = sem("row_number_made")
        ident_zeroed = sem("ident_zeroed")
        ident_made = sem("ident_made")
        high_split = sem("high_split")
        high_taken = sem("high_taken")
        middle_split = sem("middle_split")
        low_split = sem("low_split")
        hot_made = sem("hot_made")
        lookup_filled = sem("lookup_filled")
        vector_emptied = sem("vector_emptied")
        scalar_emptied = sem("scalar_emptied")
        gram_filled = sem("gram_filled")
        gram_emptied = sem("gram_emptied")
        products_stored = sem("products_stored")
        inter_loaded = sem("inter_loaded")
        dense_copied = sem("dense_copied")
        dense_weight_added = sem("dense_weight_added")
        mlp_filled = sem("mlp_filled")
        mlp_emptied = sem("mlp_emptied")
        y_stored = sem("y_stored")

        STORES, LOADS = GROUP, PAIR_CHUNKS + 1
        WEIGHTS = 6

        def empty_lookup(engine, copy, slab, fill):
            done = vector_emptied if by_vector(fill) else scalar_emptied
            engine.wait_ge(lookup_filled, total(slab, LOOKUP_FILLS, fill + 1))
            bank = lookup[fill % LOOKUP_BANKS]
            if fill < HOT_FILLS:
                first = SLOTS + 2 * fill
                src = bank[:, :].rearrange("p (f s) -> p f s", f=2)
                dst = emb[:, :, :, first:first + 2].rearrange("p h s f -> p f (h s)")
            else:
                h, b = divmod(fill - HOT_FILLS, TILE_FILLS)
                if b == 0 and not is_first(slab):
                    engine.wait_ge(dense_copied, total(slab, 1))
                n = min(PER_BANK, SLOTS - b * PER_BANK)
                src = bank[:, 0:n * TILE].rearrange("p (f s) -> p f s", f=n)
                dst = emb[:, h, :, b * PER_BANK:b * PER_BANK + n].rearrange("p s f -> p f s")
            copy(dst, src).then_inc(done, 1)

        def lookup_complete(engine, slab, fill):
            engine.wait_ge(vector_emptied, total(slab, emptied(LOOKUP_FILLS - 1, True), emptied(fill, True)))
            engine.wait_ge(scalar_emptied, total(slab, emptied(LOOKUP_FILLS - 1, False), emptied(fill, False)))

        block = ctx.enter_context(nc.Block())

        @block.sync
        def _(sp):
            def load_slab_inputs(slab, h):
                at = total(slab, SLAB, h * TILE)
                if not is_first(slab):
                    sp.wait_ge(gathered[h], total(slab, 16 * GATHERED))
                sp.dma_start(idx[h][:, :], ids[bass.ds(at, TILE), :]).then_inc(idx_loaded[h], 16)
                if not is_first(slab):
                    sp.wait_ge(lookup_filled, total(later(slab, -1), LOOKUP_FILLS, HOT_FILLS + (h + 1) * TILE_FILLS))
                sp.dma_start(rows[h][:, 0:EMBED], dense[bass.ds(at, TILE), :]).then_inc(dense_loaded[h], 16)

            def load_hot_ids(slab):
                sp.dma_start(hot_ids_i[:, :, :],
                             hot_ids[:, bass.ds(total(slab, SLAB), SLAB)].partition_broadcast(128)
                             ).then_inc(hot_ids_loaded, 16)

            def bounce(slab):
                sp.wait_ge(gram_emptied, total(slab, GRAM_FILLS, GRAM_FILLS))
                for j in range(GROUP):
                    lo, hi = j * FEATURES, (j + 1) * FEATURES
                    sp.dma_start(scratch[:, j * GROUPS:(j + 1) * GROUPS].rearrange("(f g) q -> f g q", f=FEATURES),
                                 stage[lo:hi, lo * GROUPS:hi * GROUPS].rearrange("f (g q) -> f g q", g=FEATURES)
                                 ).then_inc(products_stored, 16)
                sp.wait_ge(products_stored, total(later(slab, 1), 16 * STORES))
                per = PAIR_CHUNK // REACH
                for c in range(PAIR_CHUNKS):
                    n = min(per, FEATURES - 1 - c * per)
                    first = (FEATURES + 1) * c * per + 1
                    src = bass.AP(scratch.tensor, first * SLAB,
                                  [[(FEATURES + 1) * SLAB, n], [SLAB, REACH], [1, SLAB]])
                    sp.dma_start(inter[0:n * REACH, c, :], src).then_inc(inter_loaded, 16)
                src = bass.AP(scratch.tensor, (REACH + 1) * SLAB, [[(FEATURES + 1) * SLAB, REACH], [1, SLAB]])
                sp.dma_start(inter[PAIR_CHUNK - REACH:PAIR_CHUNK, PAIR_CHUNKS - 1, :], src).then_inc(inter_loaded, 16)

            def slab_steps(slab, last):
                if not last:
                    sp.wait_ge(hot_ids_converted, total(slab, 1, 1))
                    load_hot_ids(later(slab, 1))
                    for h in range(SLAB_TILES):
                        load_slab_inputs(later(slab, 1), h)
                bounce(slab)

            for h in range(SLAB_TILES):
                load_slab_inputs(FIRST, h)
            load_hot_ids(FIRST)
            for t in range(1, ONE_HOT, 2):
                sp.dma_start(raw[t], tables[ONE_HOT_TABLES[t]].rearrange("(p k) d -> p (k d)", k=ROW_CHUNKS)
                             ).then_inc(raw_loaded[t], 16)
            sp.dma_start(w1p[:, :, :], w_inter.rearrange("(c p) n -> p c n", p=PAIR_CHUNK)).then_inc(weights_loaded, 16)
            sp.dma_start(w1d2[:, :, :], w_dense.rearrange("(c p) n -> p c n", p=EMBED)).then_inc(weights_loaded, 16)
            sp.dma_start(w2s[:, :, :], w2.rearrange("(c p) n -> p c n", p=128)).then_inc(weights_loaded, 16)
            sp.dma_start(w3s[:, :], w3).then_inc(weights_loaded, 16)
            sp.dma_start(b1s[:, :], b1).then_inc(weights_loaded, 16)
            sp.dma_start(b2s[:, :], b2).then_inc(weights_loaded, 16)
            with sp.Fori(0, SLABS - 1) as i:
                slab_steps((i, 0), False)
            slab_steps(LAST, True)
            sp.wait_ge(mlp_emptied, SLABS * MLP_FILLS)
            sp.dma_start(out, y[:, :]).then_inc(y_stored, 16)
            sp.wait_ge(y_stored, 16)

        @block.gpsimd
        def _(pool):
            def gather_tile(slab, h):
                pool.wait_ge(idx_loaded[h], total(slab, 16, 16))
                if not is_first(slab):
                    pool.wait_ge(lookup_filled, total(later(slab, -1), LOOKUP_FILLS, HOT_FILLS + (h + 1) * TILE_FILLS))
                pool.nop(nofuse=True)
                for n, f in enumerate(GATHER_TABLES):
                    nc.gpsimd.indirect_dma_start(
                        rows[h][:, (1 + n) * EMBED:(2 + n) * EMBED], None, tables[f],
                        bass.IndirectOffsetOnAxis(idx[h][:, f:f + 1], axis=0)).then_inc(gathered[h], 16)

            gather_tile(FIRST, 0)
            nc.gpsimd.iota(row_number[:, :], pattern=[[1, ROW_CHUNKS]], base=0, channel_multiplier=ROW_CHUNKS,
                           allow_small_or_imprecise_dtypes=True).then_inc(row_number_made, 1)
            nc.gpsimd.memset(ident[:, :], 0.0).then_inc(ident_zeroed, 1)
            pool.wait_ge(ident_zeroed, 1)
            nc.gpsimd.affine_select(out=ident[:, :], in_=ident[:, :], compare_op=ALU.not_equal, fill=1.0,
                                    base=0, pattern=[[-1, 128]], channel_multiplier=1).then_inc(ident_made, 1)
            gather_tile(FIRST, 1)
            with pool.Fori(0, SLABS - 1) as i:
                for h in range(SLAB_TILES):
                    gather_tile((i, 1), h)

        @block.scalar
        def _(act):
            def mlp_evacuate(slab, fill):
                act.wait_ge(mlp_filled, total(slab, MLP_FILLS, fill + 1))
                bank = mlp[fill % MLP_BANKS]
                if fill < H1C:
                    ins = nc.scalar.activation(h1[:, fill, :], bank[:, 0:SLAB], ACT.Relu, bias=b1s[:, fill:fill + 1])
                elif fill < H1C + H2C:
                    m = fill - H1C
                    ins = nc.scalar.activation(h2[:, m, :], bank[:, 0:SLAB], ACT.Relu, bias=b2s[:, m:m + 1])
                else:
                    ins = nc.scalar.copy(y[:, bass.ds(total(slab, SLAB_TILES), SLAB_TILES)], bank[:, 0:SLAB_TILES])
                ins.then_inc(mlp_emptied, 1)

            def empty(slab, fill):
                if not by_vector(fill):
                    empty_lookup(act, lambda dst, src: nc.scalar.copy(dst, src), slab, fill)

            def gram_evacuate(slab, h):
                for b in range(GRAM_TILE_FILLS):
                    fill = h * GRAM_TILE_FILLS + b
                    act.wait_ge(gram_filled, total(slab, GRAM_FILLS, fill + 1))
                    src = gram[fill % GRAM_BANKS][0:BLOCK, 0:4 * BLOCK].rearrange("p (q c) -> p q c", q=4)
                    dst = stage_v[0:BLOCK, :, h, 4 * b:4 * b + 4].rearrange("p c q -> p q c")
                    nc.scalar.copy(dst, src).then_inc(gram_emptied, 1)

            def slab_steps(slab, first):
                for fill in range(HOT_FILLS + TILE_FILLS):
                    empty(slab, fill)
                if not first:
                    for fill in range(H1C):
                        mlp_evacuate(later(slab, -1), fill)
                    act.wait_ge(products_stored, total(slab, 16 * STORES))
                else:
                    act.wait_ge(low_split, ONE_HOT)
                gram_evacuate(slab, 0)
                for fill in range(HOT_FILLS + TILE_FILLS, LOOKUP_FILLS):
                    empty(slab, fill)
                if not first:
                    for fill in range(H1C, MLP_FILLS):
                        mlp_evacuate(later(slab, -1), fill)
                gram_evacuate(slab, 1)

            for t in range(0, ONE_HOT, 2):
                act.dma_start(raw[t], tables[ONE_HOT_TABLES[t]].rearrange("(p k) d -> p (k d)", k=ROW_CHUNKS)
                              ).then_inc(raw_loaded[t], 16)

            def split_middle(t):
                act.wait_ge(high_taken, t + 1)
                nc.scalar.copy(part[t][1][:, :, :], raw[t]).then_inc(middle_split, 1)

            for t in range(ONE_HOT):
                act.wait_ge(raw_loaded[t], 16)
                nc.scalar.copy(part[t][0][:, :, :], raw[t]).then_inc(high_split, 1)
                if t:
                    split_middle(t - 1)
            split_middle(ONE_HOT - 1)
            act.wait_ge(weights_loaded, 16 * WEIGHTS)
            slab_steps(FIRST, True)
            with act.Fori(0, SLABS - 1) as i:
                slab_steps((i, 1), False)
            for fill in range(MLP_FILLS):
                mlp_evacuate(LAST, fill)

        @block.vector
        def _(dve):
            def empty(slab, fill):
                if by_vector(fill):
                    empty_lookup(dve, lambda dst, src: nc.vector.tensor_copy(dst, src), slab, fill)

            def convert_hot_ids(slab):
                dve.wait_ge(hot_ids_loaded, total(slab, 16, 16))
                nc.vector.tensor_copy(hot_ids_h[:, :, :], hot_ids_i[:, :, :]).then_inc(hot_ids_converted, 1)
                dve.wait_ge(hot_ids_converted, total(slab, 1, 1))

            def make_hot(t):
                for k in range(ROW_CHUNKS):
                    last = nc.vector.tensor_scalar(hot[t][:, k, :], hot_ids_h[:, t, :], row_number[:, k:k + 1], None,
                                                   ALU.is_equal)
                last.then_inc(hot_made, 1)

            def copy_dense(slab):
                dve.wait_ge(vector_emptied, total(later(slab, 1), emptied(LOOKUP_FILLS - 1, True)))
                if not is_first(slab):
                    dve.wait_ge(mlp_filled, total(later(slab, -1), MLP_FILLS, H1C))
                nc.vector.tensor_copy(dense_t[:, :, :, :],
                                      emb[:, :, :, 0:1].rearrange("p h (q j) o -> p j h (q o)", j=GROUP)
                                      ).then_inc(dense_copied, 1)

            def slab_steps(slab, last):
                for fill in range(HOT_FILLS + TILE_FILLS):
                    empty(slab, fill)
                if not last:
                    convert_hot_ids(later(slab, 1))
                    dve.wait_ge(lookup_filled, total(slab, LOOKUP_FILLS, HOT_FILLS))
                    for t in range(ONE_HOT):
                        make_hot(t)
                for fill in range(HOT_FILLS + TILE_FILLS, LOOKUP_FILLS):
                    empty(slab, fill)
                copy_dense(slab)

            def split_low(t):
                dve.wait_ge(middle_split, t + 1)
                nc.vector.tensor_tensor(part[t][2][:, :, :].rearrange("p k d -> p (k d)"), raw[t],
                                        part[t][1][:, :, :].rearrange("p k d -> p (k d)"), ALU.subtract
                                        ).then_inc(low_split, 1)

            convert_hot_ids(FIRST)
            dve.wait_ge(row_number_made, 1)
            for t in range(ONE_HOT):
                dve.wait_ge(high_split, t + 1)
                nc.vector.tensor_tensor(raw[t], raw[t], part[t][0][:, :, :].rearrange("p k d -> p (k d)"),
                                        ALU.subtract).then_inc(high_taken, 1)
                make_hot(t)
                split_low(t)
            dve.wait_ge(weights_loaded, 16 * WEIGHTS)
            nc.vector.tensor_tensor(w1d[:, :], w1d2[:, 0, :], w1d2[:, 1, :], ALU.add).then_inc(dense_weight_added, 1)
            slab_steps(FIRST, False)
            with dve.Fori(0, SLABS - 2) as i:
                slab_steps((i, 1), False)
            slab_steps(LAST, True)

        @block.tensor
        def _(pe):
            def bank_free(slab, fill):
                back, prev = previous_user(fill, LOOKUP_FILLS, LOOKUP_BANKS)
                if back and is_first(slab):
                    return
                vector = by_vector(prev)
                pe.wait_ge(vector_emptied if vector else scalar_emptied,
                           total(later(slab, -back), emptied(LOOKUP_FILLS - 1, vector), emptied(prev, vector)))

            def hot_lookups(slab):
                for fill in range(HOT_FILLS):
                    bank_free(slab, fill)
                    for i in range(2):
                        t = 2 * fill + i
                        pe.wait_ge(hot_made, total(slab, ONE_HOT, t + 1))
                        if is_first(slab):
                            pe.wait_ge(low_split, t + 1)
                        dst = lookup[fill % LOOKUP_BANKS][:, i * SLAB:(i + 1) * SLAB]
                        for k in range(ROW_CHUNKS):
                            for p in range(3):
                                last = nc.tensor.matmul(dst, part[t][p][:, k, :], hot[t][0:ROW_PARTS, k, :],
                                                        start=(k == 0 and p == 0),
                                                        stop=(k == ROW_CHUNKS - 1 and p == 2))
                    last.then_inc(lookup_filled, 1)

            def transposes(slab, h):
                pe.wait_ge(gathered[h], total(later(slab, 1), 16 * GATHERED))
                pe.wait_ge(dense_loaded[h], total(slab, 16, 16))
                for b in range(TILE_FILLS):
                    fill = HOT_FILLS + h * TILE_FILLS + b
                    bank_free(slab, fill)
                    n = min(PER_BANK, SLOTS - b * PER_BANK)
                    for i in range(n):
                        f = b * PER_BANK + i
                        last = nc.tensor.transpose(lookup[fill % LOOKUP_BANKS][:, i * TILE:(i + 1) * TILE],
                                                   rows[h][:, f * EMBED:(f + 1) * EMBED], ident[:, :])
                    last.then_inc(lookup_filled, 1)

            def self_products(slab, h):
                lookup_complete(pe, slab, HOT_FILLS + (h + 1) * TILE_FILLS - 1)
                for b in range(GRAM_TILE_FILLS):
                    fill = h * GRAM_TILE_FILLS + b
                    back, prev = previous_user(fill, GRAM_FILLS, GRAM_BANKS)
                    if not (back and is_first(slab)):
                        pe.wait_ge(gram_emptied, total(later(slab, -back), GRAM_FILLS, prev + 1))
                    for i in range(4):
                        q = 4 * b + i
                        four = emb[:, h, q * GROUP:(q + 1) * GROUP, :].rearrange("p j f -> p (j f)")
                        last = nc.tensor.matmul(gram[fill % GRAM_BANKS][0:BLOCK, i * BLOCK:(i + 1) * BLOCK],
                                                four, four, start=True, stop=True)
                    last.then_inc(gram_filled, 1)

            def mlp_bank_free(slab, fill):
                back, prev = previous_user(fill, MLP_FILLS, MLP_BANKS)
                if not back:
                    pe.wait_ge(mlp_emptied, total(slab, MLP_FILLS, prev + 1))

            def layer1(slab):
                pe.wait_ge(dense_copied, total(slab, 1, 1))
                pe.wait_ge(inter_loaded, total(later(slab, 1), 16 * LOADS))
                for m in range(H1C):
                    mlp_bank_free(slab, m)
                    dst = mlp[m % MLP_BANKS][:, 0:SLAB]
                    cols = slice(m * 128, (m + 1) * 128)
                    nc.tensor.matmul(dst, w1d[:, cols], dense_t[:, :, :, :].rearrange("p j h q -> p (j h q)"),
                                     start=True, stop=False)
                    for c in range(PAIR_CHUNKS):
                        last = nc.tensor.matmul(dst, w1p[:, c, cols], inter[:, c, :],
                                                start=False, stop=(c == PAIR_CHUNKS - 1))
                    last.then_inc(mlp_filled, 1)

            def layers23(slab):
                for m in range(H2C):
                    fill = H1C + m
                    mlp_bank_free(slab, fill)
                    for c in range(H1C):
                        if m == 0:
                            pe.wait_ge(mlp_emptied, total(slab, MLP_FILLS, c + 1))
                        last = nc.tensor.matmul(mlp[fill % MLP_BANKS][:, 0:SLAB], w2s[:, c, m * 128:(m + 1) * 128],
                                                h1[:, c, :], start=(c == 0), stop=(c == H1C - 1))
                    last.then_inc(mlp_filled, 1)
                pe.wait_ge(mlp_emptied, total(slab, MLP_FILLS, H1C + H2C))
                bank = mlp[(MLP_FILLS - 1) % MLP_BANKS]
                for h in range(SLAB_TILES):
                    for c in range(H2C):
                        last = nc.tensor.matmul(bank[:, h:h + 1], h2[:, c, h * TILE:(h + 1) * TILE],
                                                w3s[:, c:c + 1], start=(c == 0), stop=(c == H2C - 1))
                last.then_inc(mlp_filled, 1)

            def slab_steps(slab, first):
                hot_lookups(slab)
                transposes(slab, 0)
                if not first:
                    layer1(later(slab, -1))
                self_products(slab, 0)
                transposes(slab, 1)
                if not first:
                    layers23(later(slab, -1))
                self_products(slab, 1)

            pe.wait_ge(ident_made, 1)
            pe.wait_ge(dense_weight_added, 1)
            slab_steps(FIRST, True)
            with pe.Fori(0, SLABS - 1) as i:
                slab_steps((i, 1), False)
            layer1(LAST)
            layers23(LAST)


def kernel(**inputs):
    import numpy as np
    import concourse.bacc as bacc
    from concourse.bass_utils import run_bass_kernel_spmd as run

    nc = bacc.Bacc("TRN2", target_bir_lowering=False, num_devices=1)
    arrays = {}

    def given(name, a):
        a = np.ascontiguousarray(a)
        arrays[name] = a
        return nc.dram_tensor(name, a.shape, mybir.dt.from_np(a.dtype), kind="ExternalInput").ap()

    w1 = np.asarray(inputs["W_top1"])
    ids = np.asarray(inputs["ids"])
    dense = given("dense", inputs["r_dense_features"])
    ids_d = given("ids", ids)
    hot_ids = given("hot_ids", ids.T[ONE_HOT_TABLES])
    tables = [given(f"tbl_{f}", inputs[f"tbl_{f}"]) for f in range(SPARSE)]
    w_inter = given("w_inter", w1[EMBED:EMBED + PAIRS][pair_weights_order()])
    w_dense = given("w_dense", np.concatenate([w1[:EMBED], w1[EMBED + PAIRS:]]))
    b1 = given("b1", np.asarray(inputs["b_top1"]).reshape(-1, 128).T)
    w2 = given("w2", inputs["W_top2"])
    b2 = given("b2", np.asarray(inputs["b_top2"]).reshape(-1, 128).T)
    w3 = given("w3", np.asarray(inputs["W_top3"]).reshape(-1, 128).T)
    out = nc.dram_tensor("out", (128, SLABS * SLAB_TILES), mybir.dt.float32, kind="ExternalOutput").ap()
    build(nc, dense, ids_d, hot_ids, tables, w_inter, w_dense, b1, w2, b2, w3, out)
    r = run(nc, [arrays], core_ids=[0])
    got = r.results[0]["out"]
    got = got.reshape(GROUP // 2, SLAB_TILES, QUARTER, SLABS, 2).transpose(3, 1, 2, 4, 0)
    return np.ascontiguousarray(got).reshape(BATCH, 1)
```

```python
import concourse.bass as bass
from concourse import mybir
from contextlib import ExitStack

BATCH = 2048
EMBED = 128
VOCAB = [1000, 1000, 1000, 125000, 1250, 1000, 1000, 12500, 1000, 1250, 12500, 1000, 1250,
         1250, 12500, 12500, 1250, 12500, 1000, 1000, 1250, 12500, 12500, 12500, 1250, 1250]
SPARSE = len(VOCAB)
FEATURES = SPARSE + 1
PAIRS = FEATURES * (FEATURES - 1) // 2
HIDDEN1, HIDDEN2 = 512, 256

ONE_HOT = 8
ROWS = 1000
ROW_PARTS = 125
ROW_CHUNKS = ROWS // ROW_PARTS
ONE_HOT_TABLES = [f for f, v in enumerate(VOCAB) if v == ROWS][:ONE_HOT]
GATHER_TABLES = [f for f in range(SPARSE) if f not in ONE_HOT_TABLES]
GATHERED = len(GATHER_TABLES)
SLOTS = 1 + GATHERED
FEATURE_ORDER = [0] + [1 + f for f in GATHER_TABLES] + [1 + f for f in ONE_HOT_TABLES]

TILE = 128
SLAB_TILES = 2
SLAB = TILE * SLAB_TILES
SLABS = BATCH // SLAB
GROUP = 4
BLOCK = GROUP * FEATURES
QUARTER = TILE // GROUP
GROUPS = SLAB_TILES * QUARTER

REACH = FEATURES // 2
PAIR_ROWS = [(FEATURES + 1) * f + k for f in range(FEATURES - 1) for k in range(1, REACH + 1)]
PAIR_ROWS += [(FEATURES + 1) * f + REACH + 1 for f in range(REACH)]
PAIR_CHUNK = 9 * REACH
PAIR_CHUNKS = PAIRS // PAIR_CHUNK


def triu_index(a, b):
    return a * FEATURES - a * (a + 1) // 2 + b - a - 1


def pair_weights_order():
    order = []
    for row in PAIR_ROWS:
        a, b = FEATURE_ORDER[row // FEATURES], FEATURE_ORDER[row % FEATURES]
        order.append(triu_index(min(a, b), max(a, b)))
    return order


LOOKUP_BANKS, GRAM_BANKS, MLP_BANKS = 3, 3, 2
PER_BANK = 4
HOT_FILLS = ONE_HOT
TILE_FILLS = -(-SLOTS // PER_BANK)
LOOKUP_FILLS = HOT_FILLS + SLAB_TILES * TILE_FILLS
GRAM_TILE_FILLS = QUARTER // 4
GRAM_FILLS = SLAB_TILES * GRAM_TILE_FILLS
MLP_FILLS = HIDDEN1 // 128 + HIDDEN2 // 128 + 1
HOT_BUFFERS = 2
RAW_BUFFERS = 6


FIRST, LAST = (0, 0), (0, SLABS - 1)


def is_first(slab):
    return isinstance(slab[0], int) and sum(slab) == 0


def is_last(slab):
    return isinstance(slab[0], int) and slab == LAST


def later(slab, n):
    return slab[0], slab[1] + n


def total(slab, per, n=0):
    base = slab[1] * per + n
    return base if isinstance(slab[0], int) else slab[0] * per + base


def tile_fill(h, b):
    return HOT_FILLS + h * TILE_FILLS + b


def by_vector(fill):
    return fill >= HOT_FILLS and (fill - HOT_FILLS) % TILE_FILLS % 2 == 0


def emptied(fill, vector):
    return sum(by_vector(i) == vector for i in range(fill + 1))


def previous_user(fill, fills, banks):
    if fill >= banks:
        return 0, fill - banks
    return 1, max(i for i in range(fills) if i % banks == fill % banks)


def build(nc, dense, ids, hot_ids, tables, w_inter, w_dense, b1, w2, b2, w3, out):
    f32, f32r, i32 = mybir.dt.float32, mybir.dt.float32r, mybir.dt.int32
    f16 = mybir.dt.float16
    ALU, ACT = mybir.AluOpType, mybir.ActivationFunctionType
    H1C, H2C = HIDDEN1 // 128, HIDDEN2 // 128

    with ExitStack() as ctx:
        def sb(name, shape, dt):
            return ctx.enter_context(nc.sbuf_tensor(name, shape, dt))

        def sem(name):
            return ctx.enter_context(nc.semaphore(name))

        idx = [sb(f"idx{h}", [TILE, SPARSE], i32) for h in range(SLAB_TILES)]
        rows = [sb(f"rows{h}", [TILE, SLOTS * EMBED], f32) for h in range(SLAB_TILES)]
        emb = sb("emb", [EMBED, SLAB_TILES, TILE, FEATURES], f32)
        hot_ids_i = sb("hot_ids_i", [128, ONE_HOT, SLAB], i32)
        hot_ids_h = sb("hot_ids_h", [128, ONE_HOT, SLAB], f16)
        row_number = sb("row_number", [128, ROW_CHUNKS], f32)
        hot = [sb(f"hot{t}", [128, ROW_CHUNKS, SLAB], f32r) for t in range(HOT_BUFFERS)]
        table_high = [sb(f"table_high{t}", [ROW_PARTS, ROW_CHUNKS * EMBED], f32r) for t in range(ONE_HOT)]
        table_low = [sb(f"table_low{t}", [ROW_PARTS, ROW_CHUNKS * EMBED], f32r) for t in range(ONE_HOT)]
        stage = sb("stage", [128, BLOCK * GROUPS], f32)
        stage_v = stage[:, :].rearrange("p (c h q) -> p c h q", c=BLOCK, h=SLAB_TILES)
        raw_cols = ROW_CHUNKS * EMBED
        assert RAW_BUFFERS * raw_cols <= BLOCK * GROUPS
        raw = [stage[0:ROW_PARTS, (t % RAW_BUFFERS) * raw_cols:(t % RAW_BUFFERS + 1) * raw_cols]
               for t in range(ONE_HOT)]
        dense_high = sb("dense_high", [EMBED, GROUP, SLAB_TILES, QUARTER], f32r)
        dense_low = sb("dense_low", [EMBED, GROUP, SLAB_TILES, QUARTER], f32r)
        inter = sb("inter", [PAIR_CHUNK, PAIR_CHUNKS, SLAB], f32)
        inter_high = sb("inter_high", [PAIR_CHUNK, PAIR_CHUNKS, SLAB], f32r)
        inter_low = sb("inter_low", [PAIR_CHUNK, PAIR_CHUNKS, SLAB], f32r)
        h1 = sb("h1", [128, H1C, SLAB], f32)
        h2 = sb("h2", [128, H2C, SLAB], f32)
        y = sb("y", [128, SLABS * SLAB_TILES], f32)
        w1p = rows[1][0:PAIR_CHUNK, 0:PAIR_CHUNKS * HIDDEN1]
        w1d = h1[:, :, :].rearrange("p c n -> p (c n)")
        assert H1C * SLAB == 2 * HIDDEN1
        w1p_high = sb("w1p_high", [PAIR_CHUNK, PAIR_CHUNKS * HIDDEN1], f32r)
        w1p_low = sb("w1p_low", [PAIR_CHUNK, PAIR_CHUNKS * HIDDEN1], f32r)
        w1d_high = sb("w1d_high", [EMBED, HIDDEN1], f32r)
        w1d_low = sb("w1d_low", [EMBED, HIDDEN1], f32r)
        w2s = sb("w2s", [128, H1C, HIDDEN2], f32)
        w3s = sb("w3s", [128, H2C], f32)
        b1s = sb("b1s", [128, H1C], f32)
        b2s = sb("b2s", [128, H2C], f32)
        ident = sb("ident", [128, 128], f32)
        scratch = nc.dram_tensor("pair_products", (FEATURES * FEATURES, SLAB), f32, kind="Internal").ap()

        lookup = [ctx.enter_context(nc.psum_tensor(f"lookup{i}", [128, 512], f32)) for i in range(LOOKUP_BANKS)]
        gram = [ctx.enter_context(nc.psum_tensor(f"gram{i}", [128, 512], f32)) for i in range(GRAM_BANKS)]
        mlp = [ctx.enter_context(nc.psum_tensor(f"mlp{i}", [128, 512], f32)) for i in range(MLP_BANKS)]

        idx_loaded = [sem(f"idx_loaded{h}") for h in range(SLAB_TILES)]
        dense_loaded = [sem(f"dense_loaded{h}") for h in range(SLAB_TILES)]
        gathered = [sem(f"gathered{h}") for h in range(SLAB_TILES)]
        raw_loaded = [sem(f"raw_loaded{t}") for t in range(ONE_HOT)]
        w1_loaded = sem("w1_loaded")
        w1d_added = sem("w1d_added")
        w1_high_split = sem("w1_high_split")
        w1_low_split = sem("w1_low_split")
        weights_loaded = sem("weights_loaded")
        hot_ids_loaded = sem("hot_ids_loaded")
        hot_ids_converted = sem("hot_ids_converted")
        row_number_made = sem("row_number_made")
        ident_zeroed = sem("ident_zeroed")
        ident_made = sem("ident_made")
        high_split = sem("high_split")
        low_split = sem("low_split")
        hot_made = sem("hot_made")
        lookup_filled = sem("lookup_filled")
        vector_emptied = sem("vector_emptied")
        scalar_emptied = sem("scalar_emptied")
        gram_filled = sem("gram_filled")
        gram_emptied = sem("gram_emptied")
        products_stored = sem("products_stored")
        inter_loaded = sem("inter_loaded")
        inter_high_split = sem("inter_high_split")
        inter_split = sem("inter_split")
        dense_high_copied = sem("dense_high_copied")
        dense_copied = sem("dense_copied")
        mlp_filled = sem("mlp_filled")
        mlp_emptied = sem("mlp_emptied")
        y_stored = sem("y_stored")

        STORES, LOADS = GROUP, PAIR_CHUNKS + 1
        WEIGHTS = 4

        def copy_lookup(copy, fill):
            bank = lookup[fill % LOOKUP_BANKS]
            if fill < HOT_FILLS:
                return copy(emb[:, :, :, SLOTS + fill:SLOTS + fill + 1].rearrange("p h s f -> p (h s f)"),
                            bank[:, 0:SLAB])
            h, b = divmod(fill - HOT_FILLS, TILE_FILLS)
            n = min(PER_BANK, SLOTS - b * PER_BANK)
            return copy(emb[:, h, :, b * PER_BANK:b * PER_BANK + n].rearrange("p s f -> p f s"),
                        bank[:, 0:n * TILE].rearrange("p (f s) -> p f s", f=n))

        block = ctx.enter_context(nc.Block())

        @block.sync
        def _(sp):
            def load_ids(slab, h):
                sp.wait_ge(gathered[h], total(slab, 16 * GATHERED))
                sp.dma_start(idx[h][:, :], ids[bass.ds(total(slab, SLAB, h * TILE), TILE), :]).then_inc(idx_loaded[h], 16)

            def load_dense(slab, h):
                if not is_first(slab):
                    sp.wait_ge(lookup_filled, total(later(slab, -1), LOOKUP_FILLS, tile_fill(h + 1, 0)))
                elif h == 1:
                    sp.wait_ge(w1_low_split, 2)
                sp.dma_start(rows[h][:, 0:EMBED],
                             dense[bass.ds(total(slab, SLAB, h * TILE), TILE), :]).then_inc(dense_loaded[h], 16)

            def load_hot_ids(slab):
                sp.dma_start(hot_ids_i[:, :, :],
                             hot_ids[:, bass.ds(total(slab, SLAB), SLAB)].partition_broadcast(128)
                             ).then_inc(hot_ids_loaded, 16)

            def load_table(t):
                sp.dma_start(raw[t], tables[ONE_HOT_TABLES[t]].rearrange("(p k) d -> p (k d)", k=ROW_CHUNKS)
                             ).then_inc(raw_loaded[t], 16)

            def bounce(slab):
                sp.wait_ge(gram_emptied, total(slab, GRAM_FILLS, GRAM_FILLS))
                for j in range(GROUP):
                    lo, hi = j * FEATURES, (j + 1) * FEATURES
                    sp.dma_start(scratch[:, j * GROUPS:(j + 1) * GROUPS].rearrange("(f g) q -> f g q", f=FEATURES),
                                 stage[lo:hi, lo * GROUPS:hi * GROUPS].rearrange("f (g q) -> f g q", g=FEATURES)
                                 ).then_inc(products_stored, 16)
                sp.wait_ge(products_stored, total(later(slab, 1), 16 * STORES))
                per = PAIR_CHUNK // REACH
                for c in range(PAIR_CHUNKS):
                    n = min(per, FEATURES - 1 - c * per)
                    first = (FEATURES + 1) * c * per + 1
                    src = bass.AP(scratch.tensor, first * SLAB,
                                  [[(FEATURES + 1) * SLAB, n], [SLAB, REACH], [1, SLAB]])
                    sp.dma_start(inter[0:n * REACH, c, :], src).then_inc(inter_loaded, 16)
                src = bass.AP(scratch.tensor, (REACH + 1) * SLAB, [[(FEATURES + 1) * SLAB, REACH], [1, SLAB]])
                sp.dma_start(inter[PAIR_CHUNK - REACH:PAIR_CHUNK, PAIR_CHUNKS - 1, :], src).then_inc(inter_loaded, 16)

            def slab_steps(slab):
                if not is_last(slab):
                    sp.wait_ge(hot_ids_converted, total(slab, 1, 1))
                    load_hot_ids(later(slab, 1))
                    for h in range(SLAB_TILES):
                        load_ids(later(slab, 1), h)
                        load_dense(later(slab, 1), h)
                bounce(slab)

            sp.dma_start(idx[0][:, :], ids[0:TILE, :]).then_inc(idx_loaded[0], 16)
            sp.dma_start(idx[1][:, :], ids[TILE:2 * TILE, :]).then_inc(idx_loaded[1], 16)
            load_hot_ids(FIRST)
            load_table(0)
            sp.dma_start(w1p.rearrange("p (c n) -> p c n", c=PAIR_CHUNKS),
                         w_inter.rearrange("(c p) n -> p c n", p=PAIR_CHUNK)).then_inc(w1_loaded, 16)
            sp.dma_start(w1d.rearrange("p (c n) -> p c n", c=2),
                         w_dense.rearrange("(c p) n -> p c n", p=EMBED)).then_inc(w1_loaded, 16)
            load_dense(FIRST, 0)
            for t in range(1, min(RAW_BUFFERS, ONE_HOT)):
                load_table(t)
            sp.dma_start(w2s[:, :, :], w2.rearrange("(c p) n -> p c n", p=128)).then_inc(weights_loaded, 16)
            sp.dma_start(w3s[:, :], w3).then_inc(weights_loaded, 16)
            sp.dma_start(b1s[:, :], b1).then_inc(weights_loaded, 16)
            sp.dma_start(b2s[:, :], b2).then_inc(weights_loaded, 16)
            load_dense(FIRST, 1)
            for t in range(RAW_BUFFERS, ONE_HOT):
                sp.wait_ge(low_split, t - RAW_BUFFERS + 1)
                load_table(t)
            with sp.Fori(0, SLABS - 1) as i:
                slab_steps((i, 0))
            slab_steps(LAST)
            sp.wait_ge(mlp_emptied, SLABS * MLP_FILLS)
            sp.dma_start(out, y[:, :]).then_inc(y_stored, 16)
            sp.wait_ge(y_stored, 16)

        @block.gpsimd
        def _(pool):
            def gather_tile(slab, h):
                pool.wait_ge(idx_loaded[h], total(slab, 16, 16))
                if not is_first(slab):
                    pool.wait_ge(lookup_filled, total(later(slab, -1), LOOKUP_FILLS, tile_fill(h + 1, 0)))
                elif h == 1:
                    pool.wait_ge(w1_low_split, 2)
                pool.nop(nofuse=True)
                for n, f in enumerate(GATHER_TABLES):
                    nc.gpsimd.indirect_dma_start(
                        rows[h][:, (1 + n) * EMBED:(2 + n) * EMBED], None, tables[f],
                        bass.IndirectOffsetOnAxis(idx[h][:, f:f + 1], axis=0)).then_inc(gathered[h], 16)

            nc.gpsimd.iota(row_number[:, :], pattern=[[1, ROW_CHUNKS]], base=0, channel_multiplier=ROW_CHUNKS,
                           allow_small_or_imprecise_dtypes=True).then_inc(row_number_made, 1)
            nc.gpsimd.memset(ident[:, :], 0.0).then_inc(ident_zeroed, 1)
            pool.wait_ge(ident_zeroed, 1)
            nc.gpsimd.affine_select(out=ident[:, :], in_=ident[:, :], compare_op=ALU.not_equal, fill=1.0,
                                    base=0, pattern=[[-1, 128]], channel_multiplier=1).then_inc(ident_made, 1)
            for h in range(SLAB_TILES):
                gather_tile(FIRST, h)
            with pool.Fori(0, SLABS - 1) as i:
                for h in range(SLAB_TILES):
                    gather_tile((i, 1), h)

        @block.scalar
        def _(act):
            def mlp_evacuate(slab, fill):
                act.wait_ge(mlp_filled, total(slab, MLP_FILLS, fill + 1))
                bank = mlp[fill % MLP_BANKS]
                if fill < H1C:
                    ins = nc.scalar.activation(h1[:, fill, :], bank[:, 0:SLAB], ACT.Relu, bias=b1s[:, fill:fill + 1])
                elif fill < H1C + H2C:
                    m = fill - H1C
                    ins = nc.scalar.activation(h2[:, m, :], bank[:, 0:SLAB], ACT.Relu, bias=b2s[:, m:m + 1])
                else:
                    ins = nc.scalar.copy(y[:, bass.ds(total(slab, SLAB_TILES), SLAB_TILES)], bank[:, 0:SLAB_TILES])
                ins.then_inc(mlp_emptied, 1)

            def empty(slab, *fills):
                for fill in fills:
                    if not by_vector(fill):
                        act.wait_ge(lookup_filled, total(slab, LOOKUP_FILLS, fill + 1))
                        copy_lookup(nc.scalar.copy, fill).then_inc(scalar_emptied, 1)

            def empty_tile(slab, h, *banks):
                empty(slab, *(tile_fill(h, b) for b in banks))

            def gram_evacuate(slab, h):
                for b in range(GRAM_TILE_FILLS):
                    fill = h * GRAM_TILE_FILLS + b
                    act.wait_ge(gram_filled, total(slab, GRAM_FILLS, fill + 1))
                    src = gram[fill % GRAM_BANKS][0:BLOCK, 0:4 * BLOCK].rearrange("p (q c) -> p q c", q=4)
                    dst = stage_v[0:BLOCK, :, h, 4 * b:4 * b + 4].rearrange("p c q -> p q c")
                    nc.scalar.copy(dst, src).then_inc(gram_emptied, 1)

            def slab_steps(slab):
                def mlp_of_previous(*fills):
                    if not is_first(slab):
                        for fill in fills:
                            mlp_evacuate(later(slab, -1), fill)

                empty(slab, *range(HOT_FILLS))
                empty_tile(slab, 0, 0, 1)
                mlp_of_previous(0)
                empty_tile(slab, 0, 2)
                mlp_of_previous(1)
                empty_tile(slab, 0, *range(3, TILE_FILLS))
                mlp_of_previous(2)
                if is_first(slab):
                    act.wait_ge(low_split, ONE_HOT)
                else:
                    act.wait_ge(products_stored, total(slab, 16 * STORES))
                gram_evacuate(slab, 0)
                if is_last(slab):
                    mlp_of_previous(*range(3, MLP_FILLS))
                    empty_tile(slab, 1, *range(TILE_FILLS))
                else:
                    empty_tile(slab, 1, 0, 1)
                    mlp_of_previous(3)
                    empty_tile(slab, 1, 2, 3)
                    mlp_of_previous(4)
                    empty_tile(slab, 1, *range(4, TILE_FILLS))
                    mlp_of_previous(5)
                gram_evacuate(slab, 1)
                if not is_last(slab):
                    mlp_of_previous(6)

            for t in range(ONE_HOT):
                act.wait_ge(raw_loaded[t], 16)
                nc.scalar.copy(table_high[t][:, :], raw[t]).then_inc(high_split, 1)
                if t == 0:
                    act.wait_ge(w1_loaded, 32)
                    nc.scalar.copy(w1p_high[:, :], w1p).then_inc(w1_high_split, 1)
                    act.wait_ge(w1d_added, 1)
                    nc.scalar.copy(w1d_high[:, :], w1d[:, 0:HIDDEN1]).then_inc(w1_high_split, 1)
            act.wait_ge(weights_loaded, 16 * WEIGHTS)
            slab_steps(FIRST)
            with act.Fori(0, SLABS - 2) as i:
                slab_steps((i, 1))
            slab_steps(LAST)
            for fill in range(MLP_FILLS):
                mlp_evacuate(LAST, fill)

        @block.vector
        def _(dve):
            def empty(slab, *fills):
                for fill in fills:
                    if by_vector(fill):
                        dve.wait_ge(lookup_filled, total(slab, LOOKUP_FILLS, fill + 1))
                        if fill in (tile_fill(0, 0), tile_fill(1, 0)) and not is_first(slab):
                            dve.wait_ge(dense_copied, total(slab, 1))
                        copy_lookup(nc.vector.tensor_copy, fill).then_inc(vector_emptied, 1)

            def convert_hot_ids(slab):
                dve.wait_ge(hot_ids_loaded, total(slab, 16, 16))
                if not is_first(slab):
                    dve.wait_ge(hot_made, total(slab, ONE_HOT))
                nc.vector.tensor_copy(hot_ids_h[:, :, :], hot_ids_i[:, :, :]).then_inc(hot_ids_converted, 1)
                dve.wait_ge(hot_ids_converted, total(slab, 1, 1))

            def make_hot(t):
                for k in range(ROW_CHUNKS):
                    last = nc.vector.tensor_scalar(hot[t % HOT_BUFFERS][:, k, :], hot_ids_h[:, t, :],
                                                   row_number[:, k:k + 1], None, ALU.is_equal)
                last.then_inc(hot_made, 1)

            def split_low(t):
                dve.wait_ge(high_split, t + 1)
                nc.vector.tensor_tensor(table_low[t][:, :], raw[t], table_high[t][:, :], ALU.subtract).then_inc(low_split, 1)

            def split_inter(slab):
                dve.wait_ge(inter_loaded, total(later(slab, 1), 16 * LOADS))
                nc.vector.tensor_copy(inter_high[:, :, :], inter[:, :, :]).then_inc(inter_high_split, 1)
                dve.wait_ge(inter_high_split, total(slab, 1, 1))
                nc.vector.tensor_tensor(inter_low[:, :, :], inter[:, :, :], inter_high[:, :, :],
                                        ALU.subtract).then_inc(inter_split, 1)

            def copy_dense(slab):
                dve.wait_ge(vector_emptied, total(slab, emptied(LOOKUP_FILLS - 1, True), emptied(tile_fill(1, 0), True)))
                if not is_first(slab):
                    dve.wait_ge(mlp_filled, total(later(slab, -1), MLP_FILLS, H1C))
                src = emb[:, :, :, 0:1].rearrange("p h (q j) o -> p j h (q o)", j=GROUP)
                nc.vector.tensor_copy(dense_high[:, :, :, :], src).then_inc(dense_high_copied, 1)
                dve.wait_ge(dense_high_copied, total(slab, 1, 1))
                for h in range(SLAB_TILES):
                    last = nc.vector.tensor_tensor(dense_low[:, :, h, :], src[:, :, h, :], dense_high[:, :, h, :],
                                                   ALU.subtract)
                last.then_inc(dense_copied, 1)

            def slab_steps(slab):
                for t in range(HOT_BUFFERS, ONE_HOT):
                    if is_first(slab):
                        split_low(t)
                    dve.wait_ge(lookup_filled, total(slab, LOOKUP_FILLS, t - HOT_BUFFERS + 1))
                    make_hot(t)
                if not is_first(slab):
                    split_inter(later(slab, -1))
                empty(slab, *(tile_fill(0, b) for b in range(TILE_FILLS)))
                if not is_last(slab):
                    convert_hot_ids(later(slab, 1))
                    for t in range(HOT_BUFFERS):
                        dve.wait_ge(lookup_filled, total(slab, LOOKUP_FILLS, HOT_FILLS))
                        make_hot(t)
                empty(slab, *(tile_fill(1, b) for b in range(TILE_FILLS)))
                copy_dense(slab)

            convert_hot_ids(FIRST)
            dve.wait_ge(row_number_made, 1)
            for t in range(HOT_BUFFERS):
                make_hot(t)
                split_low(t)
                if t == 0:
                    dve.wait_ge(w1_loaded, 32)
                    nc.vector.tensor_tensor(w1d[:, 0:HIDDEN1], w1d[:, 0:HIDDEN1], w1d[:, HIDDEN1:2 * HIDDEN1],
                                            ALU.add).then_inc(w1d_added, 1)
                    dve.wait_ge(w1_high_split, 2)
                    nc.vector.tensor_tensor(w1p_low[:, :], w1p, w1p_high[:, :], ALU.subtract).then_inc(w1_low_split, 1)
                    nc.vector.tensor_tensor(w1d_low[:, :], w1d[:, 0:HIDDEN1], w1d_high[:, :],
                                            ALU.subtract).then_inc(w1_low_split, 1)
            slab_steps(FIRST)
            with dve.Fori(0, SLABS - 2) as i:
                slab_steps((i, 1))
            slab_steps(LAST)
            split_inter(LAST)

        @block.tensor
        def _(pe):
            def bank_free(slab, fill):
                back, prev = previous_user(fill, LOOKUP_FILLS, LOOKUP_BANKS)
                if not (back and is_first(slab)):
                    vector = by_vector(prev)
                    pe.wait_ge(vector_emptied if vector else scalar_emptied,
                               total(later(slab, -back), emptied(LOOKUP_FILLS - 1, vector), emptied(prev, vector)))

            def hot_lookups(slab):
                for t in range(ONE_HOT):
                    bank_free(slab, t)
                    pe.wait_ge(hot_made, total(slab, ONE_HOT, t + 1))
                    if is_first(slab):
                        pe.wait_ge(low_split, t + 1)
                    for k in range(ROW_CHUNKS):
                        for part in (table_high, table_low):
                            last = nc.tensor.matmul(lookup[t % LOOKUP_BANKS][:, 0:SLAB],
                                                    part[t][:, k * EMBED:(k + 1) * EMBED],
                                                    hot[t % HOT_BUFFERS][0:ROW_PARTS, k, :],
                                                    start=(k == 0 and part is table_high),
                                                    stop=(k == ROW_CHUNKS - 1 and part is table_low))
                    last.then_inc(lookup_filled, 1)

            def transposes(slab, h, *banks):
                pe.wait_ge(gathered[h], total(later(slab, 1), 16 * GATHERED))
                pe.wait_ge(dense_loaded[h], total(slab, 16, 16))
                for b in banks:
                    fill = tile_fill(h, b)
                    bank_free(slab, fill)
                    for i in range(min(PER_BANK, SLOTS - b * PER_BANK)):
                        f = b * PER_BANK + i
                        last = nc.tensor.transpose(lookup[fill % LOOKUP_BANKS][:, i * TILE:(i + 1) * TILE],
                                                   rows[h][:, f * EMBED:(f + 1) * EMBED], ident[:, :])
                    last.then_inc(lookup_filled, 1)

            def self_products(slab, h):
                for filled, vector in ((vector_emptied, True), (scalar_emptied, False)):
                    pe.wait_ge(filled, total(slab, emptied(LOOKUP_FILLS - 1, vector),
                                             emptied(tile_fill(h + 1, 0) - 1, vector)))
                for b in range(GRAM_TILE_FILLS):
                    fill = h * GRAM_TILE_FILLS + b
                    back, prev = previous_user(fill, GRAM_FILLS, GRAM_BANKS)
                    if not (back and is_first(slab)):
                        pe.wait_ge(gram_emptied, total(later(slab, -back), GRAM_FILLS, prev + 1))
                    for i in range(4):
                        q = 4 * b + i
                        four = emb[:, h, q * GROUP:(q + 1) * GROUP, :].rearrange("p j f -> p (j f)")
                        last = nc.tensor.matmul(gram[fill % GRAM_BANKS][0:BLOCK, i * BLOCK:(i + 1) * BLOCK],
                                                four, four, start=True, stop=True)
                    last.then_inc(gram_filled, 1)

            def mlp_bank_free(slab, fill):
                back, prev = previous_user(fill, MLP_FILLS, MLP_BANKS)
                if not back:
                    pe.wait_ge(mlp_emptied, total(slab, MLP_FILLS, prev + 1))

            def layer1(slab, *chunks):
                pe.wait_ge(w1_low_split, 2)
                pe.wait_ge(dense_copied, total(slab, 1, 1))
                pe.wait_ge(inter_split, total(slab, 1, 1))
                for m in chunks:
                    mlp_bank_free(slab, m)
                    dst = mlp[m % MLP_BANKS][:, 0:SLAB]
                    inputs = [(w1d_high, w1d_low, m * 128, dense_high[:, :, :, :].rearrange("p j h q -> p (j h q)"),
                               dense_low[:, :, :, :].rearrange("p j h q -> p (j h q)"))]
                    inputs += [(w1p_high, w1p_low, c * HIDDEN1 + m * 128, inter_high[:, c, :], inter_low[:, c, :])
                               for c in range(PAIR_CHUNKS)]
                    for c, (w_high, w_low, col, x_high, x_low) in enumerate(inputs):
                        nc.tensor.matmul(dst, w_high[:, col:col + 128], x_high, start=(c == 0), stop=False)
                        nc.tensor.matmul(dst, w_high[:, col:col + 128], x_low, start=False, stop=False)
                        last = nc.tensor.matmul(dst, w_low[:, col:col + 128], x_high,
                                                start=False, stop=(c == PAIR_CHUNKS))
                    last.then_inc(mlp_filled, 1)

            def layer2(slab, *chunks):
                pe.wait_ge(mlp_emptied, total(slab, MLP_FILLS, H1C))
                for m in chunks:
                    fill = H1C + m
                    mlp_bank_free(slab, fill)
                    for c in range(H1C):
                        last = nc.tensor.matmul(mlp[fill % MLP_BANKS][:, 0:SLAB], w2s[:, c, m * 128:(m + 1) * 128],
                                                h1[:, c, :], start=(c == 0), stop=(c == H1C - 1))
                    last.then_inc(mlp_filled, 1)

            def layer3(slab):
                pe.wait_ge(mlp_emptied, total(slab, MLP_FILLS, H1C + H2C))
                bank = mlp[(MLP_FILLS - 1) % MLP_BANKS]
                for h in range(SLAB_TILES):
                    for c in range(H2C):
                        last = nc.tensor.matmul(bank[:, h:h + 1], h2[:, c, h * TILE:(h + 1) * TILE],
                                                w3s[:, c:c + 1], start=(c == 0), stop=(c == H2C - 1))
                last.then_inc(mlp_filled, 1)

            def slab_steps(slab):
                def of_previous(layer, *chunks):
                    if not is_first(slab):
                        layer(later(slab, -1), *chunks)

                hot_lookups(slab)
                transposes(slab, 0, 0, 1)
                of_previous(layer1, 0)
                transposes(slab, 0, 2)
                of_previous(layer1, 1)
                transposes(slab, 0, *range(3, TILE_FILLS))
                of_previous(layer1, 2)
                self_products(slab, 0)
                if is_last(slab):
                    of_previous(layer1, 3)
                    of_previous(layer2, 0, 1)
                    of_previous(layer3)
                    transposes(slab, 1, *range(TILE_FILLS))
                else:
                    transposes(slab, 1, 0, 1)
                    of_previous(layer1, 3)
                    transposes(slab, 1, 2, 3)
                    of_previous(layer2, 0)
                    transposes(slab, 1, *range(4, TILE_FILLS))
                    of_previous(layer2, 1)
                self_products(slab, 1)
                if not is_last(slab):
                    of_previous(layer3)

            pe.wait_ge(ident_made, 1)
            slab_steps(FIRST)
            with pe.Fori(0, SLABS - 2) as i:
                slab_steps((i, 1))
            slab_steps(LAST)
            layer1(LAST, 0, 1, 2, 3)
            layer2(LAST, 0, 1)
            layer3(LAST)


def kernel(**inputs):
    import numpy as np
    import concourse.bacc as bacc
    from concourse.bass_utils import run_bass_kernel_spmd as run

    nc = bacc.Bacc("TRN2", target_bir_lowering=False, num_devices=1)
    arrays = {}

    def given(name, a):
        a = np.ascontiguousarray(a)
        arrays[name] = a
        return nc.dram_tensor(name, a.shape, mybir.dt.from_np(a.dtype), kind="ExternalInput").ap()

    w1 = np.asarray(inputs["W_top1"])
    ids = np.asarray(inputs["ids"])
    dense = given("dense", inputs["r_dense_features"])
    ids_d = given("ids", ids)
    hot_ids = given("hot_ids", ids.T[ONE_HOT_TABLES])
    tables = [given(f"tbl_{f}", inputs[f"tbl_{f}"]) for f in range(SPARSE)]
    w_inter = given("w_inter", w1[EMBED:EMBED + PAIRS][pair_weights_order()])
    w_dense = given("w_dense", np.concatenate([w1[:EMBED], w1[EMBED + PAIRS:]]))
    b1 = given("b1", np.asarray(inputs["b_top1"]).reshape(-1, 128).T)
    w2 = given("w2", inputs["W_top2"])
    b2 = given("b2", np.asarray(inputs["b_top2"]).reshape(-1, 128).T)
    w3 = given("w3", np.asarray(inputs["W_top3"]).reshape(-1, 128).T)
    out = nc.dram_tensor("out", (128, SLABS * SLAB_TILES), mybir.dt.float32, kind="ExternalOutput").ap()
    build(nc, dense, ids_d, hot_ids, tables, w_inter, w_dense, b1, w2, b2, w3, out)
    r = run(nc, [arrays], core_ids=[0])
    got = r.results[0]["out"]
    got = got.reshape(GROUP // 2, SLAB_TILES, QUARTER, SLABS, 2).transpose(3, 1, 2, 4, 0)
    return np.ascontiguousarray(got).reshape(BATCH, 1)
```

```python
import concourse.bass as bass
from concourse import mybir
from contextlib import ExitStack

BATCH = 2048
EMBED = 128
VOCAB = [1000, 1000, 1000, 125000, 1250, 1000, 1000, 12500, 1000, 1250, 12500, 1000, 1250,
         1250, 12500, 12500, 1250, 12500, 1000, 1000, 1250, 12500, 12500, 12500, 1250, 1250]
SPARSE = len(VOCAB)
FEATURES = SPARSE + 1
PAIRS = FEATURES * (FEATURES - 1) // 2
HIDDEN1, HIDDEN2 = 512, 256

ONE_HOT = 8
ROWS = 1000
ROW_PARTS = 125
ROW_CHUNKS = ROWS // ROW_PARTS
ONE_HOT_TABLES = [f for f, v in enumerate(VOCAB) if v == ROWS][:ONE_HOT]
GATHER_TABLES = [f for f in range(SPARSE) if f not in ONE_HOT_TABLES]
GATHERED = len(GATHER_TABLES)
SLOTS = 1 + GATHERED
FEATURE_ORDER = [0] + [1 + f for f in GATHER_TABLES] + [1 + f for f in ONE_HOT_TABLES]

TILE = 128
SLAB_TILES = 2
SLAB = TILE * SLAB_TILES
SLABS = BATCH // SLAB
GROUP = 4
RIGHT = FEATURES - 1
BLOCK = GROUP * FEATURES
BLOCK_COLS = GROUP * RIGHT
QUARTER = TILE // GROUP
GROUPS = SLAB_TILES * QUARTER

REACH = FEATURES // 2
PAIR_ROWS = [(RIGHT + 1) * f + k - 1 for f in range(FEATURES - 1) for k in range(1, REACH + 1)]
PAIR_ROWS += list(range(REACH, RIGHT))
PAIR_CHUNK = 9 * REACH
PAIR_CHUNKS = PAIRS // PAIR_CHUNK


def triu_index(a, b):
    return a * FEATURES - a * (a + 1) // 2 + b - a - 1


def pair_weights_order():
    order = []
    for row in PAIR_ROWS:
        a, b = FEATURE_ORDER[row // RIGHT], FEATURE_ORDER[row % RIGHT + 1]
        order.append(triu_index(min(a, b), max(a, b)))
    return order


LOOKUP_BANKS, GRAM_BANKS, MLP_BANKS = 3, 3, 2
PER_BANK = 4
HOT_FILLS = ONE_HOT
TILE_FILLS = -(-SLOTS // PER_BANK)
FIRST_GATHERS = (TILE_FILLS - 1) * PER_BANK - 1
REST_GATHERS = GATHERED - FIRST_GATHERS
LOOKUP_FILLS = HOT_FILLS + SLAB_TILES * TILE_FILLS
GRAM_TILE_FILLS = QUARTER // 4
GRAM_FILLS = SLAB_TILES * GRAM_TILE_FILLS
MLP_FILLS = HIDDEN1 // 128 + HIDDEN2 // 128 + 1
HOT_BUFFERS = 2
HALF = ROW_CHUNKS // 2
IDS_AT_A_TIME = ONE_HOT // 2
H1_BUFFERS = 2
RAW_BUFFERS = 4


FIRST, LAST = (0, 0), (0, SLABS - 1)


def is_first(slab):
    return isinstance(slab[0], int) and sum(slab) == 0


def is_last(slab):
    return isinstance(slab[0], int) and slab == LAST


def later(slab, n):
    return slab[0], slab[1] + n


def total(slab, per, n=0):
    base = slab[1] * per + n
    return base if isinstance(slab[0], int) else slab[0] * per + base


def tile_fill(h, b):
    return HOT_FILLS + h * TILE_FILLS + b


def by_vector(fill):
    return fill >= HOT_FILLS and (fill - HOT_FILLS) % TILE_FILLS % 2 == 0


def emptied(fill, vector):
    return sum(by_vector(i) == vector for i in range(fill + 1))


def previous_user(fill, fills, banks):
    if fill >= banks:
        return 0, fill - banks
    return 1, max(i for i in range(fills) if i % banks == fill % banks)


def build(nc, dense, ids, hot_ids, tables, w_inter, w_dense, w2, unit_columns, out):
    f32, f32r, i32 = mybir.dt.float32, mybir.dt.float32r, mybir.dt.int32
    f16 = mybir.dt.float16
    ALU, ACT = mybir.AluOpType, mybir.ActivationFunctionType
    H1C, H2C = HIDDEN1 // 128, HIDDEN2 // 128

    with ExitStack() as ctx:
        def sb(name, shape, dt):
            return ctx.enter_context(nc.sbuf_tensor(name, shape, dt))

        def sem(name):
            return ctx.enter_context(nc.semaphore(name))

        idx_both = sb("idx", [TILE, SLAB_TILES, SPARSE], i32)
        idx = [idx_both[:, h, :] for h in range(SLAB_TILES)]
        rows = [sb(f"rows{h}", [TILE, SLOTS * EMBED], f32) for h in range(SLAB_TILES)]
        emb = sb("emb", [EMBED, SLAB_TILES, TILE, FEATURES], f32)
        hot_ids_i = sb("hot_ids_i", [128, IDS_AT_A_TIME, SLAB], i32)
        hot_ids_h = sb("hot_ids_h", [128, ONE_HOT, SLAB], f16)
        first_row = sb("first_row", [128, 1], f32)
        hot = [sb(f"hot{t}", [128, ROW_CHUNKS, SLAB], f32r) for t in range(HOT_BUFFERS)]
        table_high = [sb(f"table_high{t}", [ROW_PARTS, ROW_CHUNKS * EMBED], f32r) for t in range(ONE_HOT)]
        table_low = [sb(f"table_low{t}", [ROW_PARTS, ROW_CHUNKS * EMBED], f32r) for t in range(ONE_HOT)]
        stage = sb("stage", [128, BLOCK_COLS * GROUPS], f32)
        stage_v = stage[:, :].rearrange("p (c h q) -> p c h q", c=BLOCK_COLS, h=SLAB_TILES)
        raw_cols = ROW_CHUNKS * EMBED
        raw = [stage[0:ROW_PARTS, (t % RAW_BUFFERS) * raw_cols:(t % RAW_BUFFERS + 1) * raw_cols]
               for t in range(ONE_HOT)]
        w1p_at, w2_at = RAW_BUFFERS * raw_cols, RAW_BUFFERS * raw_cols + PAIR_CHUNKS * HIDDEN1
        assert w2_at + H1C * HIDDEN2 <= BLOCK_COLS * GROUPS
        w1p = stage[0:PAIR_CHUNK, w1p_at:w2_at]
        w2r = stage[:, w2_at:w2_at + H1C * HIDDEN2]
        dense_high = sb("dense_high", [EMBED, GROUP, SLAB_TILES, QUARTER], f32r)
        dense_low = sb("dense_low", [EMBED, GROUP, SLAB_TILES, QUARTER], f32r)
        inter = sb("inter", [PAIR_CHUNK, PAIR_CHUNKS, SLAB], f32)
        inter_high = sb("inter_high", [PAIR_CHUNK, PAIR_CHUNKS, SLAB], f32r)
        inter_low = sb("inter_low", [PAIR_CHUNK, PAIR_CHUNKS, SLAB], f32r)
        hidden = sb("hidden", [128, H1_BUFFERS + H2C, SLAB], f32)
        h1, h2 = hidden[:, 0:H1_BUFFERS, :], hidden[:, H1_BUFFERS:H1_BUFFERS + H2C, :]
        h1_high = sb("h1_high", [128, H1C, SLAB], f32r)
        h1_low = sb("h1_low", [128, H1C, SLAB], f32r)
        y = sb("y", [128, SLABS * SLAB_TILES], f32)
        w1d = hidden[:, :, :].rearrange("p c n -> p (c n)")
        assert (H1_BUFFERS + H2C) * SLAB == 2 * HIDDEN1
        w2_high = sb("w2_high", [128, H1C * HIDDEN2], f32r)
        w2_low = sb("w2_low", [128, H1C * HIDDEN2], f32r)
        w1p_high = sb("w1p_high", [PAIR_CHUNK, PAIR_CHUNKS * HIDDEN1], f32r)
        w1p_low = sb("w1p_low", [PAIR_CHUNK, PAIR_CHUNKS * HIDDEN1], f32r)
        w1d_high = sb("w1d_high", [EMBED, HIDDEN1], f32r)
        w1d_low = sb("w1d_low", [EMBED, HIDDEN1], f32r)
        columns = sb("columns", [128, H1C + 2 * H2C], f32)
        b1s, b2s, w3s = columns[:, 0:H1C], columns[:, H1C:H1C + H2C], columns[:, H1C + H2C:]
        ident = sb("ident", [128, 128], f32)
        scratch = nc.dram_tensor("pair_products", (FEATURES * RIGHT, SLAB), f32, kind="Internal").ap()

        lookup = [ctx.enter_context(nc.psum_tensor(f"lookup{i}", [128, 512], f32)) for i in range(LOOKUP_BANKS)]
        gram = [ctx.enter_context(nc.psum_tensor(f"gram{i}", [128, 512], f32)) for i in range(GRAM_BANKS)]
        mlp = [ctx.enter_context(nc.psum_tensor(f"mlp{i}", [128, 512], f32)) for i in range(MLP_BANKS)]

        idx_loaded = [sem(f"idx_loaded{h}") for h in range(SLAB_TILES)]
        dense_loaded = [sem(f"dense_loaded{h}") for h in range(SLAB_TILES)]
        first_gathered = [sem(f"first_gathered{h}") for h in range(SLAB_TILES)]
        rest_gathered = [sem(f"rest_gathered{h}") for h in range(SLAB_TILES)]
        raw_loaded = [sem(f"raw_loaded{t}") for t in range(ONE_HOT)]
        w1p_loaded = sem("w1p_loaded")
        w1p_high_split = sem("w1p_high_split")
        w1p_low_split = sem("w1p_low_split")
        w1d_loaded = sem("w1d_loaded")
        w1d_added = sem("w1d_added")
        w1d_high_split = sem("w1d_high_split")
        w1d_low_split = sem("w1d_low_split")
        w2_loaded = sem("w2_loaded")
        w2_high_split = sem("w2_high_split")
        w2_low_split = sem("w2_low_split")
        columns_loaded = sem("columns_loaded")
        hot_ids_loaded = sem("hot_ids_loaded")
        hot_ids_converted = sem("hot_ids_converted")
        first_row_made = sem("first_row_made")
        ident_zeroed = sem("ident_zeroed")
        ident_made = sem("ident_made")
        high_split = sem("high_split")
        low_split = sem("low_split")
        hot_made = sem("hot_made")
        first_half_used = sem("first_half_used")
        lookup_filled = sem("lookup_filled")
        vector_emptied = sem("vector_emptied")
        scalar_emptied = sem("scalar_emptied")
        gram_filled = sem("gram_filled")
        gram_emptied = sem("gram_emptied")
        products_stored = sem("products_stored")
        inter_loaded = [sem(f"inter_loaded{c}") for c in range(PAIR_CHUNKS)]
        inter_high_split = sem("inter_high_split")
        inter_split = sem("inter_split")
        h1_high_split = sem("h1_high_split")
        h1_split = sem("h1_split")
        dense_high_copied = sem("dense_high_copied")
        dense_copied = sem("dense_copied")
        mlp_filled = sem("mlp_filled")
        mlp_emptied = sem("mlp_emptied")
        y_stored = sem("y_stored")

        STORES = GROUP

        def mlp_bank(slab, fill):
            return (lookup + gram + mlp)[fill] if is_last(slab) else mlp[fill % MLP_BANKS]

        def copy_lookup(copy, fill):
            bank = lookup[fill % LOOKUP_BANKS]
            if fill < HOT_FILLS:
                return copy(emb[:, :, :, SLOTS + fill:SLOTS + fill + 1].rearrange("p h s f -> p (h s f)"),
                            bank[:, 0:SLAB])
            h, b = divmod(fill - HOT_FILLS, TILE_FILLS)
            n = min(PER_BANK, SLOTS - b * PER_BANK)
            return copy(emb[:, h, :, b * PER_BANK:b * PER_BANK + n].rearrange("p s f -> p f s"),
                        bank[:, 0:n * TILE].rearrange("p (f s) -> p f s", f=n))

        block = ctx.enter_context(nc.Block())

        @block.sync
        def _(sp):
            def load_ids(slab, h):
                sp.wait_ge(first_gathered[h], total(slab, 16 * FIRST_GATHERS))
                sp.wait_ge(rest_gathered[h], total(slab, 16 * REST_GATHERS))
                sp.dma_start(idx[h][:, :], ids[bass.ds(total(slab, SLAB, h * TILE), TILE), :]).then_inc(idx_loaded[h], 16)

            def load_dense(slab, h):
                if not is_first(slab):
                    sp.wait_ge(lookup_filled, total(later(slab, -1), LOOKUP_FILLS, tile_fill(h + 1, 0)))
                sp.dma_start(rows[h][:, 0:EMBED],
                             dense[bass.ds(total(slab, SLAB, h * TILE), TILE), :]).then_inc(dense_loaded[h], 16)

            def load_hot_ids(slab, part):
                if not (is_first(slab) and part == 0):
                    sp.wait_ge(hot_ids_converted, total(slab, 2, part))
                lo = part * IDS_AT_A_TIME
                sp.dma_start(hot_ids_i[:, :, :],
                             hot_ids[lo:lo + IDS_AT_A_TIME, bass.ds(total(slab, SLAB), SLAB)].partition_broadcast(128)
                             ).then_inc(hot_ids_loaded, 16)

            def load_table(t):
                sp.dma_start(raw[t], tables[ONE_HOT_TABLES[t]].rearrange("(p k) d -> p (k d)", k=ROW_CHUNKS)
                             ).then_inc(raw_loaded[t], 16)

            def store_products(tiles):
                first, n = tiles[0], len(tiles)
                for j in range(GROUP):
                    dst = scratch[:, j * GROUPS + first * QUARTER:j * GROUPS + (first + n) * QUARTER]
                    src = stage_v[j * FEATURES:(j + 1) * FEATURES, j * RIGHT:(j + 1) * RIGHT, first:first + n, :]
                    sp.dma_start(dst.rearrange("(f g) q -> f g q", f=FEATURES),
                                 src.rearrange("f g h q -> f g (h q)")).then_inc(products_stored, 16)

            def bounce(slab):
                if is_last(slab):
                    sp.wait_ge(gram_emptied, total(slab, GRAM_FILLS, GRAM_TILE_FILLS))
                    store_products([0])
                    sp.wait_ge(gram_emptied, total(slab, GRAM_FILLS, GRAM_FILLS))
                    store_products([1])
                else:
                    sp.wait_ge(gram_emptied, total(slab, GRAM_FILLS, GRAM_FILLS))
                    store_products([0, 1])
                stored = 2 * STORES if is_last(slab) else STORES
                sp.wait_ge(products_stored, total(slab, 16 * STORES, 16 * stored))
                per = PAIR_CHUNK // REACH
                for c in range(PAIR_CHUNKS):
                    n = min(per, FEATURES - 1 - c * per)
                    src = bass.AP(scratch.tensor, (RIGHT + 1) * c * per * SLAB,
                                  [[(RIGHT + 1) * SLAB, n], [SLAB, REACH], [1, SLAB]])
                    sp.dma_start(inter[0:n * REACH, c, :], src).then_inc(inter_loaded[c], 16)
                sp.dma_start(inter[PAIR_CHUNK - REACH:PAIR_CHUNK, PAIR_CHUNKS - 1, :],
                             scratch[REACH:RIGHT, :]).then_inc(inter_loaded[PAIR_CHUNKS - 1], 16)

            def slab_steps(slab):
                if not is_last(slab):
                    load_hot_ids(later(slab, 1), 0)
                    for h in range(SLAB_TILES):
                        load_ids(later(slab, 1), h)
                        load_dense(later(slab, 1), h)
                    load_hot_ids(later(slab, 1), 1)
                bounce(slab)

            sp.dma_start(idx[0][:, :], ids[0:TILE, :]).then_inc(idx_loaded[0], 16)
            load_hot_ids(FIRST, 0)
            load_table(0)
            load_table(1)
            sp.dma_start(idx[1][:, :], ids[TILE:2 * TILE, :]).then_inc(idx_loaded[1], 16)
            load_dense(FIRST, 0)
            load_table(2)
            load_hot_ids(FIRST, 1)
            load_table(3)
            sp.dma_start(w1p.rearrange("p (c n) -> p c n", c=PAIR_CHUNKS),
                         w_inter.rearrange("(c p) n -> p c n", p=PAIR_CHUNK)).then_inc(w1p_loaded, 16)
            sp.dma_start(w2r.rearrange("p (c n) -> p c n", c=H1C),
                         w2.rearrange("(c p) n -> p c n", p=128)).then_inc(w2_loaded, 16)
            for t in range(RAW_BUFFERS, ONE_HOT):
                sp.wait_ge(low_split, t - RAW_BUFFERS + 1)
                load_table(t)
            load_dense(FIRST, 1)
            sp.dma_start(w1d.rearrange("p (c n) -> p c n", c=2),
                         w_dense.rearrange("(c p) n -> p c n", p=EMBED)).then_inc(w1d_loaded, 16)
            sp.dma_start(columns[:, :], unit_columns).then_inc(columns_loaded, 16)
            slab_steps(FIRST)
            with sp.Fori(0, SLABS - 2) as i:
                slab_steps((i, 1))
            slab_steps(LAST)
            sp.wait_ge(mlp_emptied, SLABS * MLP_FILLS)
            sp.dma_start(out, y[:, :]).then_inc(y_stored, 16)
            sp.wait_ge(y_stored, 16)

        @block.gpsimd
        def _(pool):
            def gather_tile(slab, h):
                pool.wait_ge(idx_loaded[h], total(slab, 16, 16))
                if not is_first(slab):
                    pool.wait_ge(lookup_filled, total(later(slab, -1), LOOKUP_FILLS, tile_fill(h + 1, 0)))
                pool.nop(nofuse=True)
                for n, f in enumerate(GATHER_TABLES):
                    nc.gpsimd.indirect_dma_start(
                        rows[h][:, (1 + n) * EMBED:(2 + n) * EMBED], None, tables[f],
                        bass.IndirectOffsetOnAxis(idx[h][:, f:f + 1], axis=0)).then_inc(
                        first_gathered[h] if n < FIRST_GATHERS else rest_gathered[h], 16)

            nc.gpsimd.iota(first_row[:, :], pattern=[[1, 1]], base=0, channel_multiplier=ROW_CHUNKS,
                           allow_small_or_imprecise_dtypes=True).then_inc(first_row_made, 1)
            nc.gpsimd.memset(ident[:, :], 0.0).then_inc(ident_zeroed, 1)
            pool.wait_ge(ident_zeroed, 1)
            nc.gpsimd.affine_select(out=ident[:, :], in_=ident[:, :], compare_op=ALU.not_equal, fill=1.0,
                                    base=0, pattern=[[-1, 128]], channel_multiplier=1).then_inc(ident_made, 1)
            for h in range(SLAB_TILES):
                gather_tile(FIRST, h)
            with pool.Fori(0, SLABS - 1) as i:
                for h in range(SLAB_TILES):
                    gather_tile((i, 1), h)

        @block.scalar
        def _(act):
            def mlp_evacuate(slab, fill):
                act.wait_ge(mlp_filled, total(slab, MLP_FILLS, fill + 1))
                bank = mlp_bank(slab, fill)
                if fill < H1C:
                    if fill >= H1_BUFFERS:
                        act.wait_ge(h1_split, total(slab, H1C, fill - H1_BUFFERS + 1))
                    ins = nc.scalar.activation(h1[:, fill % H1_BUFFERS, :], bank[:, 0:SLAB], ACT.Relu, bias=b1s[:, fill:fill + 1])
                elif fill < H1C + H2C:
                    m = fill - H1C
                    ins = nc.scalar.activation(h2[:, m, :], bank[:, 0:SLAB], ACT.Relu, bias=b2s[:, m:m + 1])
                else:
                    ins = nc.scalar.copy(y[:, bass.ds(total(slab, SLAB_TILES), SLAB_TILES)], bank[:, 0:SLAB_TILES])
                ins.then_inc(mlp_emptied, 1)

            def empty(slab, *fills):
                for fill in fills:
                    if not by_vector(fill):
                        act.wait_ge(lookup_filled, total(slab, LOOKUP_FILLS, fill + 1))
                        copy_lookup(nc.scalar.copy, fill).then_inc(scalar_emptied, 1)

            def empty_tile(slab, h, *banks):
                empty(slab, *(tile_fill(h, b) for b in banks))

            def gram_evacuate(slab, h):
                for b in range(GRAM_TILE_FILLS):
                    fill = h * GRAM_TILE_FILLS + b
                    act.wait_ge(gram_filled, total(slab, GRAM_FILLS, fill + 1))
                    src = gram[fill % GRAM_BANKS][0:BLOCK, 0:4 * BLOCK_COLS].rearrange("p (q c) -> p q c", q=4)
                    dst = stage_v[0:BLOCK, :, h, 4 * b:4 * b + 4].rearrange("p c q -> p q c")
                    nc.scalar.copy(dst, src).then_inc(gram_emptied, 1)

            def split_high(t):
                act.wait_ge(raw_loaded[t], 16)
                nc.scalar.copy(table_high[t][:, :], raw[t]).then_inc(high_split, 1)

            def slab_steps(slab):
                def mlp_of_previous(*fills):
                    if not is_first(slab):
                        for fill in fills:
                            mlp_evacuate(later(slab, -1), fill)

                for t in range(ONE_HOT):
                    empty(slab, t)
                    if is_first(slab) and t + LOOKUP_BANKS < ONE_HOT:
                        split_high(t + LOOKUP_BANKS)
                    elif is_first(slab) and t == ONE_HOT - LOOKUP_BANKS:
                        act.wait_ge(w1p_loaded, 16)
                        nc.scalar.copy(w1p_high[:, :], w1p).then_inc(w1p_high_split, 1)
                    elif is_first(slab) and t == ONE_HOT - LOOKUP_BANKS + 1:
                        act.wait_ge(w2_loaded, 16)
                        nc.scalar.copy(w2_high[:, :], w2r).then_inc(w2_high_split, 1)
                if is_first(slab):
                    act.wait_ge(columns_loaded, 16)
                if is_last(slab):
                    empty_tile(slab, 0, *range(TILE_FILLS))
                    mlp_of_previous(0)
                else:
                    empty_tile(slab, 0, 0, 1)
                    mlp_of_previous(0)
                    empty_tile(slab, 0, 2)
                    mlp_of_previous(1)
                    empty_tile(slab, 0, *range(3, TILE_FILLS))
                    mlp_of_previous(2)
                if is_first(slab):
                    act.wait_ge(low_split, ONE_HOT)
                    act.wait_ge(w1p_low_split, 1)
                    act.wait_ge(w2_low_split, 1)
                else:
                    act.wait_ge(products_stored, total(slab, 16 * STORES))
                gram_evacuate(slab, 0)
                if is_last(slab):
                    empty_tile(slab, 1, *range(TILE_FILLS))
                    gram_evacuate(slab, 1)
                    mlp_of_previous(*range(1, MLP_FILLS))
                else:
                    mlp_of_previous(3)
                    empty_tile(slab, 1, *range(3))
                    mlp_of_previous(4)
                    empty_tile(slab, 1, *range(3, TILE_FILLS))
                    mlp_of_previous(5)
                    gram_evacuate(slab, 1)
                    mlp_of_previous(6)

            for t in range(LOOKUP_BANKS):
                split_high(t)
            slab_steps(FIRST)
            with act.Fori(0, SLABS - 2) as i:
                slab_steps((i, 1))
            slab_steps(LAST)
            for fill in range(MLP_FILLS):
                mlp_evacuate(LAST, fill)

        @block.vector
        def _(dve):
            def empty(slab, *fills):
                for fill in fills:
                    if by_vector(fill):
                        dve.wait_ge(lookup_filled, total(slab, LOOKUP_FILLS, fill + 1))
                        if fill in (tile_fill(0, 0), tile_fill(1, 0)) and not is_first(slab):
                            dve.wait_ge(dense_copied, total(slab, 1))
                        copy_lookup(nc.vector.tensor_copy, fill).then_inc(vector_emptied, 1)

            def empty_tile(slab, h, *banks):
                empty(slab, *(tile_fill(h, b) for b in banks))

            def convert_hot_ids(slab, part):
                dve.wait_ge(hot_ids_loaded, total(slab, 2 * 16, 16 * (part + 1)))
                if not is_first(slab):
                    dve.wait_ge(hot_made, total(slab, 2 * ONE_HOT))
                lo = part * IDS_AT_A_TIME
                nc.vector.tensor_scalar(hot_ids_h[:, lo:lo + IDS_AT_A_TIME, :], hot_ids_i[:, :, :], first_row[:, 0:1], None,
                                        ALU.subtract).then_inc(hot_ids_converted, 1)
                dve.wait_ge(hot_ids_converted, total(slab, 2, part + 1))

            def make_hot(slab, t):
                for k in range(ROW_CHUNKS):
                    back, n = (0, t - HOT_BUFFERS + 1) if t >= HOT_BUFFERS else (1, ONE_HOT + t - HOT_BUFFERS + 1)
                    if not (back and is_first(slab)):
                        if k == 0:
                            dve.wait_ge(first_half_used, total(later(slab, -back), ONE_HOT, n))
                        if k == HALF:
                            dve.wait_ge(lookup_filled, total(later(slab, -back), LOOKUP_FILLS, n))
                    last = nc.vector.tensor_scalar(hot[t % HOT_BUFFERS][:, k, :], hot_ids_h[:, t, :],
                                                   float(k), None, ALU.is_equal)
                    if k % HALF == HALF - 1:
                        last.then_inc(hot_made, 1)

            def split_low(t):
                dve.wait_ge(high_split, t + 1)
                nc.vector.tensor_tensor(table_low[t][:, :], raw[t], table_high[t][:, :], ALU.subtract).then_inc(low_split, 1)

            def split_w1d():
                dve.wait_ge(w1d_loaded, 16)
                nc.vector.tensor_tensor(w1d[:, 0:HIDDEN1], w1d[:, 0:HIDDEN1], w1d[:, HIDDEN1:2 * HIDDEN1],
                                        ALU.add).then_inc(w1d_added, 1)
                dve.wait_ge(w1d_added, 1)
                nc.vector.tensor_copy(w1d_high[:, :], w1d[:, 0:HIDDEN1]).then_inc(w1d_high_split, 1)
                dve.wait_ge(w1d_high_split, 1)
                nc.vector.tensor_tensor(w1d_low[:, :], w1d[:, 0:HIDDEN1], w1d_high[:, :],
                                        ALU.subtract).then_inc(w1d_low_split, 1)

            def split_w1p_w2():
                dve.wait_ge(w1p_high_split, 1)
                nc.vector.tensor_tensor(w1p_low[:, :], w1p, w1p_high[:, :], ALU.subtract).then_inc(w1p_low_split, 1)
                dve.wait_ge(w2_high_split, 1)
                nc.vector.tensor_tensor(w2_low[:, :], w2r, w2_high[:, :], ALU.subtract).then_inc(w2_low_split, 1)

            def split_h1(slab, *chunks):
                for m in chunks:
                    dve.wait_ge(mlp_emptied, total(slab, MLP_FILLS, m + 1))
                    nc.vector.tensor_copy(h1_high[:, m, :], h1[:, m % H1_BUFFERS, :]).then_inc(h1_high_split, 1)
                    dve.wait_ge(h1_high_split, total(slab, H1C, m + 1))
                    nc.vector.tensor_tensor(h1_low[:, m, :], h1[:, m % H1_BUFFERS, :], h1_high[:, m, :],
                                            ALU.subtract).then_inc(h1_split, 1)

            def split_inter(slab):
                for c in range(PAIR_CHUNKS):
                    loads = 2 if c == PAIR_CHUNKS - 1 else 1
                    dve.wait_ge(inter_loaded[c], total(later(slab, 1), 16 * loads))
                    nc.vector.tensor_copy(inter_high[:, c, :], inter[:, c, :]).then_inc(inter_high_split, 1)
                    dve.wait_ge(inter_high_split, total(slab, PAIR_CHUNKS, c + 1))
                    nc.vector.tensor_tensor(inter_low[:, c, :], inter[:, c, :], inter_high[:, c, :],
                                            ALU.subtract).then_inc(inter_split, 1)

            def copy_dense(slab):
                dve.wait_ge(vector_emptied, total(slab, emptied(LOOKUP_FILLS - 1, True), emptied(tile_fill(1, 0), True)))
                if not is_first(slab):
                    dve.wait_ge(mlp_filled, total(later(slab, -1), MLP_FILLS, H1C))
                src = emb[:, :, :, 0:1].rearrange("p h (q j) o -> p j h (q o)", j=GROUP)
                nc.vector.tensor_copy(dense_high[:, :, :, :], src).then_inc(dense_high_copied, 1)
                dve.wait_ge(dense_high_copied, total(slab, 1, 1))
                for h in range(SLAB_TILES):
                    last = nc.vector.tensor_tensor(dense_low[:, :, h, :], src[:, :, h, :], dense_high[:, :, h, :],
                                                   ALU.subtract)
                last.then_inc(dense_copied, 1)

            def slab_steps(slab):
                def split_h1_of_previous(m):
                    if not is_first(slab):
                        split_h1(later(slab, -1), m)

                for t in range(HOT_BUFFERS, ONE_HOT):
                    if is_first(slab):
                        split_low(t)
                    make_hot(slab, t)
                if is_first(slab):
                    split_w1p_w2()
                else:
                    split_inter(later(slab, -1))
                if is_last(slab):
                    empty_tile(slab, 0, *range(TILE_FILLS))
                    split_h1_of_previous(0)
                    empty_tile(slab, 1, *range(TILE_FILLS))
                    for m in range(1, H1C):
                        split_h1_of_previous(m)
                else:
                    empty_tile(slab, 0, 0, 1, 2)
                    split_h1_of_previous(0)
                    empty_tile(slab, 0, *range(3, TILE_FILLS))
                    split_h1_of_previous(1)
                    convert_hot_ids(later(slab, 1), 0)
                    make_hot(later(slab, 1), 0)
                    split_h1_of_previous(2)
                    make_hot(later(slab, 1), 1)
                    empty_tile(slab, 1, 0)
                    split_h1_of_previous(3)
                    empty_tile(slab, 1, *range(1, TILE_FILLS))
                copy_dense(slab)
                if not is_last(slab):
                    convert_hot_ids(later(slab, 1), 1)
                if is_first(slab):
                    split_w1d()

            dve.wait_ge(first_row_made, 1)
            convert_hot_ids(FIRST, 0)
            for t in range(HOT_BUFFERS):
                make_hot(FIRST, t)
            for t in range(HOT_BUFFERS):
                split_low(t)
            convert_hot_ids(FIRST, 1)
            slab_steps(FIRST)
            with dve.Fori(0, SLABS - 2) as i:
                slab_steps((i, 1))
            slab_steps(LAST)
            split_inter(LAST)
            split_h1(LAST, *range(H1C))

        @block.tensor
        def _(pe):
            def bank_free(slab, fill):
                back, prev = previous_user(fill, LOOKUP_FILLS, LOOKUP_BANKS)
                if not (back and is_first(slab)):
                    vector = by_vector(prev)
                    pe.wait_ge(vector_emptied if vector else scalar_emptied,
                               total(later(slab, -back), emptied(LOOKUP_FILLS - 1, vector), emptied(prev, vector)))

            def hot_lookups(slab):
                for t in range(ONE_HOT):
                    bank_free(slab, t)
                    if is_first(slab):
                        pe.wait_ge(low_split, t + 1)
                    for k in range(ROW_CHUNKS):
                        if k % HALF == 0:
                            pe.wait_ge(hot_made, total(slab, 2 * ONE_HOT, 2 * t + k // HALF + 1))
                        for part in (table_high, table_low):
                            last = nc.tensor.matmul(lookup[t % LOOKUP_BANKS][:, 0:SLAB],
                                                    part[t][:, k * EMBED:(k + 1) * EMBED],
                                                    hot[t % HOT_BUFFERS][0:ROW_PARTS, k, :],
                                                    start=(k == 0 and part is table_high),
                                                    stop=(k == ROW_CHUNKS - 1 and part is table_low))
                        if k == HALF - 1:
                            last.then_inc(first_half_used, 1)
                    last.then_inc(lookup_filled, 1)

            def transposes(slab, h, *banks):
                for b in banks:
                    if b == 0:
                        pe.wait_ge(first_gathered[h], total(later(slab, 1), 16 * FIRST_GATHERS))
                        pe.wait_ge(dense_loaded[h], total(slab, 16, 16))
                    if b == TILE_FILLS - 1:
                        pe.wait_ge(rest_gathered[h], total(later(slab, 1), 16 * REST_GATHERS))
                    fill = tile_fill(h, b)
                    bank_free(slab, fill)
                    for i in range(min(PER_BANK, SLOTS - b * PER_BANK)):
                        f = b * PER_BANK + i
                        last = nc.tensor.transpose(lookup[fill % LOOKUP_BANKS][:, i * TILE:(i + 1) * TILE],
                                                   rows[h][:, f * EMBED:(f + 1) * EMBED], ident[:, :])
                    last.then_inc(lookup_filled, 1)

            def self_products(slab, h):
                for filled, vector in ((vector_emptied, True), (scalar_emptied, False)):
                    pe.wait_ge(filled, total(slab, emptied(LOOKUP_FILLS - 1, vector),
                                             emptied(tile_fill(h + 1, 0) - 1, vector)))
                for b in range(GRAM_TILE_FILLS):
                    fill = h * GRAM_TILE_FILLS + b
                    back, prev = previous_user(fill, GRAM_FILLS, GRAM_BANKS)
                    if not (back and is_first(slab)):
                        pe.wait_ge(gram_emptied, total(later(slab, -back), GRAM_FILLS, prev + 1))
                    for i in range(4):
                        q = 4 * b + i
                        four = emb[:, h, q * GROUP:(q + 1) * GROUP, :]
                        last = nc.tensor.matmul(gram[fill % GRAM_BANKS][0:BLOCK, i * BLOCK_COLS:(i + 1) * BLOCK_COLS],
                                                four.rearrange("p j f -> p (j f)"), four[:, :, 1:FEATURES],
                                                start=True, stop=True)
                    last.then_inc(gram_filled, 1)

            def mlp_bank_free(slab, fill):
                back, prev = previous_user(fill, MLP_FILLS, MLP_BANKS)
                if not (back or is_last(slab)):
                    pe.wait_ge(mlp_emptied, total(slab, MLP_FILLS, prev + 1))

            def layer1_input(m, c):
                if c == 0:
                    return (w1d_high[:, m * 128:(m + 1) * 128], w1d_low[:, m * 128:(m + 1) * 128],
                            dense_high[:, :, :, :].rearrange("p j h q -> p (j h q)"),
                            dense_low[:, :, :, :].rearrange("p j h q -> p (j h q)"))
                col = (c - 1) * HIDDEN1 + m * 128
                return (w1p_high[:, col:col + 128], w1p_low[:, col:col + 128],
                        inter_high[:, c - 1, :], inter_low[:, c - 1, :])

            def three_products(dst, w_high, w_low, x_high, x_low, start, stop):
                nc.tensor.matmul(dst, w_high, x_high, start=start, stop=False)
                nc.tensor.matmul(dst, w_high, x_low, start=False, stop=False)
                return nc.tensor.matmul(dst, w_low, x_high, start=False, stop=stop)

            def layer1_ready(slab):
                pe.wait_ge(w1p_low_split, 1)
                pe.wait_ge(w1d_low_split, 1)
                pe.wait_ge(dense_copied, total(slab, 1, 1))

            def layer1(slab, *chunks):
                layer1_ready(slab)
                for m in chunks:
                    mlp_bank_free(slab, m)
                    for c in range(1 + PAIR_CHUNKS):
                        if m == 0 and c > 0:
                            pe.wait_ge(inter_split, total(slab, PAIR_CHUNKS, c))
                        last = three_products(mlp_bank(slab, m)[:, 0:SLAB], *layer1_input(m, c),
                                              start=(c == 0), stop=(c == PAIR_CHUNKS))
                    last.then_inc(mlp_filled, 1)

            def last_layer1_dense():
                layer1_ready(LAST)
                pe.wait_ge(gram_emptied, SLABS * GRAM_FILLS)
                for m in range(H1C):
                    three_products(mlp_bank(LAST, m)[:, 0:SLAB], *layer1_input(m, 0), start=True, stop=False)

            def last_layer1_products():
                for inputs in ([1], range(2, 1 + PAIR_CHUNKS)):
                    for m in range(H1C):
                        for c in inputs:
                            if m == 0:
                                pe.wait_ge(inter_split, total(LAST, PAIR_CHUNKS, c))
                            last = three_products(mlp_bank(LAST, m)[:, 0:SLAB], *layer1_input(m, c),
                                                  start=False, stop=(c == PAIR_CHUNKS))
                        if c == PAIR_CHUNKS:
                            last.then_inc(mlp_filled, 1)

            def layer2(slab, *chunks):
                pe.wait_ge(w2_low_split, 1)
                for inputs in [[c] for c in range(H1C)] if is_last(slab) else (range(H1C - 1), [H1C - 1]):
                    for m in chunks:
                        for c in inputs:
                            if c == 0:
                                mlp_bank_free(slab, H1C + m)
                            if m == 0:
                                pe.wait_ge(h1_split, total(slab, H1C, c + 1))
                            col = c * HIDDEN2 + m * 128
                            last = three_products(mlp_bank(slab, H1C + m)[:, 0:SLAB],
                                                  w2_high[:, col:col + 128], w2_low[:, col:col + 128],
                                                  h1_high[:, c, :], h1_low[:, c, :],
                                                  start=(c == 0), stop=(c == H1C - 1))
                        if c == H1C - 1:
                            last.then_inc(mlp_filled, 1)

            def layer3(slab):
                pe.wait_ge(columns_loaded, 16)
                pe.wait_ge(mlp_emptied, total(slab, MLP_FILLS, H1C + H2C))
                bank = mlp_bank(slab, MLP_FILLS - 1)
                for h in range(SLAB_TILES):
                    for c in range(H2C):
                        last = nc.tensor.matmul(bank[:, h:h + 1], h2[:, c, h * TILE:(h + 1) * TILE],
                                                w3s[:, c:c + 1], start=(c == 0), stop=(c == H2C - 1))
                last.then_inc(mlp_filled, 1)

            def slab_steps(slab):
                def of_previous(layer, *chunks):
                    if not is_first(slab):
                        layer(later(slab, -1), *chunks)

                hot_lookups(slab)
                if is_last(slab):
                    transposes(slab, 0, *range(TILE_FILLS))
                    of_previous(layer1, 0)
                    self_products(slab, 0)
                    transposes(slab, 1, *range(TILE_FILLS))
                    self_products(slab, 1)
                    of_previous(layer1, 1, 2, 3)
                    of_previous(layer2, 0, 1)
                    last_layer1_dense()
                else:
                    transposes(slab, 0, 0, 1)
                    of_previous(layer1, 0)
                    transposes(slab, 0, 2)
                    of_previous(layer1, 1)
                    transposes(slab, 0, *range(3, TILE_FILLS))
                    of_previous(layer1, 2)
                    self_products(slab, 0)
                    of_previous(layer1, 3)
                    transposes(slab, 1, *range(3))
                    of_previous(layer2, 0)
                    transposes(slab, 1, *range(3, TILE_FILLS))
                    of_previous(layer2, 1)
                    self_products(slab, 1)
                of_previous(layer3)

            pe.wait_ge(ident_made, 1)
            slab_steps(FIRST)
            with pe.Fori(0, SLABS - 2) as i:
                slab_steps((i, 1))
            slab_steps(LAST)
            last_layer1_products()
            layer2(LAST, 0, 1)
            layer3(LAST)


def kernel(**inputs):
    import numpy as np
    import concourse.bacc as bacc
    from concourse.bass_utils import run_bass_kernel_spmd as run

    nc = bacc.Bacc("TRN2", target_bir_lowering=False, num_devices=1)
    arrays = {}

    def given(name, a):
        a = np.ascontiguousarray(a)
        arrays[name] = a
        return nc.dram_tensor(name, a.shape, mybir.dt.from_np(a.dtype), kind="ExternalInput").ap()

    w1 = np.asarray(inputs["W_top1"])
    ids = np.asarray(inputs["ids"])
    dense = given("dense", inputs["r_dense_features"])
    ids_d = given("ids", ids)
    hot_ids = given("hot_ids", ids.T[ONE_HOT_TABLES])
    tables = [given(f"tbl_{f}", inputs[f"tbl_{f}"]) for f in range(SPARSE)]
    w_inter = given("w_inter", w1[EMBED:EMBED + PAIRS][pair_weights_order()])
    w_dense = given("w_dense", np.concatenate([w1[:EMBED], w1[EMBED + PAIRS:]]))
    w2 = given("w2", inputs["W_top2"])
    unit_columns = given("unit_columns", np.concatenate(
        [np.asarray(inputs[name]).reshape(-1, 128).T for name in ("b_top1", "b_top2", "W_top3")], axis=1))
    out = nc.dram_tensor("out", (128, SLABS * SLAB_TILES), mybir.dt.float32, kind="ExternalOutput").ap()
    build(nc, dense, ids_d, hot_ids, tables, w_inter, w_dense, w2, unit_columns, out)
    r = run(nc, [arrays], core_ids=[0])
    got = r.results[0]["out"]
    got = got.reshape(GROUP // 2, SLAB_TILES, QUARTER, SLABS, 2).transpose(3, 1, 2, 4, 0)
    return np.ascontiguousarray(got).reshape(BATCH, 1)
```
